# Optimizing a Trainium2 kernel written in Bass

```python
import numpy as np
import jax
import jax.numpy as jnp

def _softmax(x, axis=-1):
    return jax.nn.softmax(x, axis=axis)

def _gelu(x):
    return jax.nn.gelu(x, approximate=True)

def _silu(x):
    return jax.nn.silu(x)

def _sigmoid(x):
    return jax.nn.sigmoid(x)

def _layernorm(x, axis=-1, eps=1e-05):
    m = jnp.mean(x, axis=axis, keepdims=True)
    v = jnp.var(x, axis=axis, keepdims=True)
    return (x - m) / jnp.sqrt(v + eps)

def _scatter_add(tgt, idx, src, axis=0):
    return tgt.at[idx].add(src)

def _segment_sum(src, seg, n):
    return jax.ops.segment_sum(src, seg, n)
kernel_name = 'mk_decoder_preln_d1_seqx_r8_ae37d6'

def setup_inputs(seed: int=0):
    np.random.seed(seed)
    _w = jnp.asarray

    def _rec_inputs():
        import jax
        import jax.numpy as jnp
        _rk = jax.random.key(seed)
        x = 7.22e-05 + 1 * jax.random.normal(jax.random.fold_in(_rk, 1), (32, 64, 512), jnp.float32)
        _lenS = 64 - jax.random.randint(jax.random.fold_in(_rk, 7), (32,), 0, max(1, 64 // 4) + 1, jnp.int32)
        _lenS2 = 64 - jax.random.randint(jax.random.fold_in(_rk, 8), (32,), 0, max(1, 64 // 4) + 1, jnp.int32)
        _ctx_4096P = jax.random.normal(jax.random.fold_in(_rk, 11), (32, 16, 512), jnp.float32)
        _ctx_4096c = jax.random.dirichlet(jax.random.fold_in(_rk, 511), 0.3 * jnp.ones((16,), jnp.float32), (32, 64))
        _ctx_4096t = jnp.einsum('bsk,bkd->bsd', _ctx_4096c, _ctx_4096P)
        _ctx_4096t = _ctx_4096t * jax.lax.rsqrt(jnp.mean(jnp.square(_ctx_4096t)) + 1e-12) * 0.953939
        ctx_4096 = 4.13588e-05 + 0.999923 * (_ctx_4096t + 0.3 * jax.random.normal(jax.random.fold_in(_rk, 611), (32, 64, 512), jnp.float32))
        return (x, ctx_4096)
    x, ctx_4096 = _rec_inputs()

    def _L0_attn_setup():
        import jax, jax.numpy as jnp
        import numpy as np
        BATCH, SEQ, HIDDEN = (2, 512, 512)
        HEADS, HEAD_DIM, BLOCK = (32, 128, 32)
        LAYER_IDX, N_LAYERS = (1, 32)
        EPS = 1e-05

        def _decays():
            base = 1.0 / 2.0 ** (8.0 / HEADS)
            exponent = jnp.arange(HEADS, dtype=jnp.float32) + 1.0
            factor = 1.0 - LAYER_IDX / (N_LAYERS - 1 + 1e-05) + 1e-05
            slope = (base ** exponent * factor)[:, None, None]
            r = jnp.arange(BLOCK, dtype=jnp.float32) + 1.0
            q_decay = jnp.exp(-slope * r[:, None])
            k_decay = jnp.exp(-slope * (BLOCK - r)[:, None])
            diff = r[:, None] - r[None, :]
            diag = slope[None] * diff[None, None]
            diag = jnp.where(diag >= 0, -diag, -jnp.inf)
            diag_decay = jnp.exp(diag)
            block_decay = jnp.exp(-slope * BLOCK)
            return (q_decay, k_decay, diag_decay, block_decay)
        key = jax.random.key(seed)
        ks = jax.random.split(key, 5)
        s = 0.02
        return {'hidden_states': jax.random.normal(ks[0], (BATCH, SEQ, HIDDEN), jnp.float32), 'qkv_w': jax.random.normal(ks[1], (3 * HEADS * HEAD_DIM, HIDDEN), jnp.float32) * s, 'out_w': jax.random.normal(ks[2], (HIDDEN, HEADS * HEAD_DIM), jnp.float32) * s, 'gate_w': jax.random.normal(ks[3], (HEADS * HEAD_DIM, HIDDEN), jnp.float32) * s, 'norm_w': jnp.ones((HEADS * HEAD_DIM,), jnp.float32)}
    _L0_attn_all = _L0_attn_setup()
    _L0_attn_in = {k: v for k, v in _L0_attn_all.items() if k in ('qkv_w', 'out_w', 'gate_w', 'norm_w')}
    del _L0_attn_all

    def _L0_xattn_setup():
        import jax, jax.numpy as jnp
        import numpy as np
        B, C, T = (4, 64, 512)
        DQK = 64
        key = jax.random.key(seed)
        ks = jax.random.split(key, 8)
        s = 1.0 / np.sqrt(C)
        return {'x': jax.random.normal(ks[0], (B, C, T), dtype=jnp.float32), 'init': jax.random.normal(ks[1], (B, C, T), dtype=jnp.float32), 'Wq': jax.random.normal(ks[2], (DQK, C), dtype=jnp.float32) * s, 'bq': jax.random.normal(ks[3], (DQK,), dtype=jnp.float32) * s, 'Wk': jax.random.normal(ks[4], (DQK, C), dtype=jnp.float32) * s, 'bk': jax.random.normal(ks[5], (DQK,), dtype=jnp.float32) * s, 'Wv': jax.random.normal(ks[6], (C, C), dtype=jnp.float32) * s, 'bv': jax.random.normal(ks[7], (C,), dtype=jnp.float32) * s}
    _L0_xattn_all = _L0_xattn_setup()
    _L0_xattn_in = {k: v for k, v in _L0_xattn_all.items() if k in ('Wq', 'bq', 'Wk', 'bk', 'Wv', 'bv')}
    del _L0_xattn_all

    def _L0_ffn_setup():
        import jax, jax.numpy as jnp
        import numpy as np
        DIM = 512
        key = jax.random.key(seed)
        x = jax.random.normal(key, (4, 512, DIM), dtype=jnp.float32)
        identity = jnp.eye(DIM, dtype=jnp.float32)
        return {'x': x, 'identity': identity}
    _L0_ffn_all = _L0_ffn_setup()
    _L0_ffn_in = {k: v for k, v in _L0_ffn_all.items() if k in ('identity',)}
    del _L0_ffn_all
    return {'x': x, 'ctx_4096': ctx_4096, 'L0_attn_qkv_w': _L0_attn_in['qkv_w'], 'L0_attn_out_w': _L0_attn_in['out_w'], 'L0_attn_gate_w': _L0_attn_in['gate_w'], 'L0_attn_norm_w': _L0_attn_in['norm_w'], 'L0_xattn_Wq': _L0_xattn_in['Wq'], 'L0_xattn_bq': _L0_xattn_in['bq'], 'L0_xattn_Wk': _L0_xattn_in['Wk'], 'L0_xattn_bk': _L0_xattn_in['bk'], 'L0_xattn_Wv': _L0_xattn_in['Wv'], 'L0_xattn_bv': _L0_xattn_in['bv'], 'L0_ffn_identity': _L0_ffn_in['identity']}

def reference(x, ctx_4096, L0_attn_qkv_w, L0_attn_out_w, L0_attn_gate_w, L0_attn_norm_w, L0_xattn_Wq, L0_xattn_bq, L0_xattn_Wk, L0_xattn_bk, L0_xattn_Wv, L0_xattn_bv, L0_ffn_identity):
    import jax
    import jax.numpy as jnp

    def _L0_attn_ref(hidden_states, qkv_w, out_w, gate_w, norm_w):
        import jax, jax.numpy as jnp
        import numpy as np
        BATCH, SEQ, HIDDEN = (2, 512, 512)
        HEADS, HEAD_DIM, BLOCK = (32, 128, 32)
        LAYER_IDX, N_LAYERS = (1, 32)
        EPS = 1e-05

        def _decays():
            base = 1.0 / 2.0 ** (8.0 / HEADS)
            exponent = jnp.arange(HEADS, dtype=jnp.float32) + 1.0
            factor = 1.0 - LAYER_IDX / (N_LAYERS - 1 + 1e-05) + 1e-05
            slope = (base ** exponent * factor)[:, None, None]
            r = jnp.arange(BLOCK, dtype=jnp.float32) + 1.0
            q_decay = jnp.exp(-slope * r[:, None])
            k_decay = jnp.exp(-slope * (BLOCK - r)[:, None])
            diff = r[:, None] - r[None, :]
            diag = slope[None] * diff[None, None]
            diag = jnp.where(diag >= 0, -diag, -jnp.inf)
            diag_decay = jnp.exp(diag)
            block_decay = jnp.exp(-slope * BLOCK)
            return (q_decay, k_decay, diag_decay, block_decay)
        b, s, _ = hidden_states.shape
        h, d, bs = (HEADS, HEAD_DIM, BLOCK)
        nb = s // bs
        q_decay, k_decay, diag_decay, block_decay = _decays()
        qkv = jax.nn.silu(hidden_states @ qkv_w.T)
        qkv = qkv.reshape(b, s, h, 3, d)
        q = jnp.moveaxis(qkv[:, :, :, 0], 2, 1)
        k = jnp.moveaxis(qkv[:, :, :, 1], 2, 1)
        v = jnp.moveaxis(qkv[:, :, :, 2], 2, 1)

        def to_blocks(x):
            return jnp.moveaxis(x.reshape(b, h, nb, bs, d), 2, 0)
        qb, kb, vb = (to_blocks(q), to_blocks(k), to_blocks(v))

        def step(kv, blk):
            cq, ck, cv = blk
            scores = jnp.einsum('bhnd,bhmd->bhnm', cq, ck) * diag_decay
            intra = jnp.einsum('bhnm,bhmd->bhnd', scores, cv)
            inter = jnp.einsum('bhnd,bhde->bhne', cq * q_decay, kv)
            kv_next = kv * block_decay + jnp.einsum('bhnd,bhne->bhde', ck * k_decay, cv)
            return (kv_next, intra + inter)
        kv0 = jnp.zeros((b, h, d, d), hidden_states.dtype)
        _, out_blocks = jax.lax.scan(step, kv0, (qb, kb, vb))
        attn = jnp.moveaxis(out_blocks, 0, 2)
        attn = attn.reshape(b, h, s, d).transpose(0, 2, 1, 3).reshape(b, s, h * d)
        xf = attn.astype(jnp.float32)
        xf = xf * jax.lax.rsqrt(jnp.mean(xf * xf, axis=-1, keepdims=True) + EPS)
        normed = norm_w * xf.astype(attn.dtype)
        gate = jax.nn.sigmoid(hidden_states @ gate_w.T)
        return gate * normed @ out_w.T

    def _L0_xattn_ref(x, init, Wq, bq, Wk, bk, Wv, bv):
        import jax, jax.numpy as jnp
        import numpy as np
        B, C, T = (4, 64, 512)
        DQK = 64
        q = jnp.einsum('dc,bct->btd', Wq, init) + bq
        k = jnp.einsum('dc,bct->bdt', Wk, init) + bk[None, :, None]
        R = jnp.einsum('btd,bds->bts', q, k)
        attention = jax.nn.softmax(R, axis=-1)
        v = jnp.einsum('oc,bct->bto', Wv, x) + bv
        out = jnp.einsum('bts,bsc->bct', attention, v)
        return out

    def _L0_ffn_ref(x, identity):
        import jax, jax.numpy as jnp
        import numpy as np
        DIM = 512
        return jnp.einsum('bsd,ed->bse', x, identity)
    x = x + _L0_attn_ref(_layernorm(x, axis=-1), L0_attn_qkv_w, L0_attn_out_w, L0_attn_gate_w, L0_attn_norm_w)
    x = x + _L0_xattn_ref(_layernorm(x, axis=-1), ctx_4096, L0_xattn_Wq, L0_xattn_bq, L0_xattn_Wk, L0_xattn_bk, L0_xattn_Wv, L0_xattn_bv)
    x = x + _L0_ffn_ref(_layernorm(x, axis=-1), L0_ffn_identity)
    return x

_drawn_inputs = setup_inputs


def setup_inputs(seed=0):
    import zlib

    import numpy as np

    out = dict(_drawn_inputs(seed))
    spreads = {'L0_attn_norm_w': (1.0, 0.2)}
    factors = {}
    for name, (base, spread) in spreads.items():
        noise = np.random.default_rng([zlib.crc32(name.encode()), seed]).standard_normal(out[name].shape)
        drawn = base * np.exp(spread * noise) if base else spread * noise
        out[name] = jnp.asarray(drawn.astype(out[name].dtype))
    for name, factor in factors.items():
        out[name] = (out[name] * factor).astype(out[name].dtype)
    return out
```

```python
from contextlib import ExitStack

import numpy as np

import concourse.bass as bass
from concourse import mybir
from concourse.alu_op_type import AluOpType as ALU

ACT = mybir.ActivationFunctionType
AX = mybir.AxisListType
F32 = mybir.dt.float32
F32R = mybir.dt.float32r

P = 128
B, SEQ, D = 32, 64, 512
TOKENS = B * SEQ
TILES = TOKENS // P
CH = D // P
HEADS, HD = 32, 128
HG = 2
GROUPS = HEADS // HG
TB = 4
BT = TOKENS // TB
TT = BT // P
EPS = 1e-5
LAYER_IDX, N_LAYERS = 1, 32


def decay_table():
    f = np.float32
    base = f(1.0 / 2.0 ** (8.0 / HEADS))
    factor = f(1.0 - LAYER_IDX / (N_LAYERS - 1 + 1e-5) + 1e-5)
    slope = (base ** (np.arange(HEADS, dtype=f) + f(1.0)) * factor).astype(np.float64)
    m = np.arange(P)[:, None, None]
    n = np.arange(P)[None, None, :]
    seen = (n >= m) & (n // SEQ == m // SEQ)
    return np.where(seen, np.exp(-slope[None, :, None] * np.maximum(n - m, 0)), 0.0).astype(f)


def decoder_layer(nc, x, ctx_in, w_qkv, w_gate, w_out, norm_w, decay, ident_in, wq_in, wk_in, wv_in, bq_in, bk_in,
                  bv_in, eye_in, out):
    with ExitStack() as both:
        def sb(stack, name, shape, dt=F32):
            return stack.enter_context(nc.sbuf_tensor(name, shape, dt))

        def sem(name):
            return both.enter_context(nc.semaphore(name))

        bank = both.enter_context(nc.psum_tensor("bank", [P, 8, 512], F32))
        attn_acc = sb(both, "attn_acc", [P, TILES, D])
        sq_acc = sb(both, "sq_acc", [P, TOKENS])
        ident = sb(both, "ident", [P, P])
        ones = sb(both, "ones", [P, 2])

        attention(nc, sb, sem, bank, attn_acc, sq_acc, ident, ones,
                  x, w_qkv, w_gate, w_out, norm_w, decay, ident_in)
        cross_and_ffn(nc, sb, sem, bank, attn_acc, sq_acc, ident, ones, x, ctx_in, wq_in, wk_in, wv_in, bq_in, bk_in,
                      bv_in, eye_in, out)


def wait_apart(eng, sem, value, passed):
    eng.wait_ge(sem, value)
    eng.sem_inc(passed, 1)


def attention(nc, sb, sem, bank, attn_acc, sq_acc, ident, ones, x, w_qkv, w_gate, w_out, norm_w, decay, ident_in):
    with ExitStack() as own:
        xn_hi = sb(own, "xn_hi", [P, CH, TOKENS], F32R)
        xn_lo = sb(own, "xn_lo", [P, CH, TOKENS], F32R)
        w_hi = sb(own, "w_hi", [P, 5, CH * HG * HD], F32R)
        w_lo = sb(own, "w_lo", [P, 5, CH * HG * HD], F32R)
        raw = sb(own, "raw", [P, 2, CH * HG * HD])
        decays = sb(own, "decays", [P, HG, P])
        normw = sb(own, "normw", [P, HEADS])
        qk = sb(own, "qk", [P, 2, HG, BT])
        v = sb(own, "v", [P, TT, HG * HD])
        scores = sb(own, "scores", [P, HG, BT])
        gate = sb(own, "gate", [P, HG, BT])
        attn = sb(own, "attn", [P, HG, BT])
        y_hi = sb(own, "y_hi", [P, HG, BT], F32R)
        y_lo = sb(own, "y_lo", [P, HG, BT], F32R)
        sq = sb(own, "sq", [P, BT])
        xn = sb(own, "xn", [P, 2, D])
        stats = sb(own, "stats", [P, 2, 6])
        mv = sb(own, "mv", [P, 2, 2])
        rstd = sb(own, "rstd", [P, 2])
        minus_half = sb(own, "minus_half", [P, 1])

        wq, wk, wv, wg, wo = range(5)

        x_landed = [sem(f"x_landed{i}") for i in range(TB)]
        const_landed = sem("const_landed")
        normw_landed = sem("normw_landed")
        consts_set = sem("consts_set")
        decay_landed = sem("decay_landed")
        raw_landed = [sem("raw_landed_a"), sem("raw_landed_b")]
        hi_cut = sem("hi_cut")
        w_ready = sem("w_ready")
        stats_done = sem("stats_done")
        var_ready = sem("var_ready")
        eps_added = sem("eps_added")
        rstd_ready = sem("rstd_ready")
        xn_ready = sem("xn_ready")
        xn_turned = sem("xn_turned")
        xn_hi_ready = sem("xn_hi_ready")
        xn_lo_ready = sem("xn_lo_ready")
        v_mm, s_mm, g_mm, pv_mm, qk_mm, out_mm = (sem(n) for n in ("v_mm", "s_mm", "g_mm", "pv_mm", "qk_mm", "out_mm"))
        v_sig, qk_sig, gate_ready, attn_ready = (sem(n) for n in ("v_sig", "qk_sig", "gate_ready", "attn_ready"))
        v_ready, qk_ready, scores_ready = (sem(n) for n in ("v_ready", "qk_ready", "scores_ready"))
        y_made, y_hi_ready, y_ready = (sem(n) for n in ("y_made", "y_hi_ready", "y_ready"))
        out_added = sem("out_added")
        sq_made, sq_added = sem("sq_made"), sem("sq_added")

        x_t = x.rearrange("b s d -> (b s) d").rearrange("(k t p) d -> k p t d", t=TT, p=P)

        with nc.Block() as block:

            @block.sync
            def _(sp):
                sp.dma_start(ident[:, :], ident_in).then_inc(const_landed, 16)
                for k in range(TB):
                    sp.dma_start(attn_acc[:, k * TT:(k + 1) * TT], x_t[k]).then_inc(x_landed[k], 16)
                sp.dma_start(raw[:, 0], w_qkv[0, 0]).then_inc(raw_landed[0], 16)
                sp.dma_start(raw[:, 1], w_qkv[0, 1]).then_inc(raw_landed[1], 16)
                sp.dma_start(normw[:, :], norm_w).then_inc(normw_landed, 16)
                sp.dma_start(decays[:, :, :], decay[:, 0:HG, :]).then_inc(decay_landed, 16)
                def rest_of_group(g):
                    sp.wait_ge(w_ready, g * 5 + (wq + 1))
                    sp.dma_start(raw[:, 0], w_qkv[g, 2]).then_inc(raw_landed[0], 16)
                    sp.wait_ge(w_ready, g * 5 + (wk + 1))
                    sp.dma_start(raw[:, 1], w_gate[g]).then_inc(raw_landed[1], 16)
                    sp.wait_ge(w_ready, g * 5 + (wv + 1))
                    sp.dma_start(raw[:, 0], w_out[g]).then_inc(raw_landed[0], 16)

                with sp.Fori(0, GROUPS - 1) as g:
                    rest_of_group(g)
                    sp.wait_ge(w_ready, g * 5 + (wo + 1))
                    sp.dma_start(raw[:, 0], w_qkv[g + 1, 0]).then_inc(raw_landed[0], 16)
                    sp.dma_start(raw[:, 1], w_qkv[g + 1, 1]).then_inc(raw_landed[1], 16)
                    sp.wait_ge(scores_ready, (g + 1) * (TB * HG))
                    sp.dma_start(decays[:, :, :], decay[:, bass.ds((g + 1) * HG, HG), :]).then_inc(decay_landed, 16)
                rest_of_group(GROUPS - 1)

            @block.gpsimd
            def _(pool):
                nc.gpsimd.memset(minus_half[:, :], -0.5).then_inc(consts_set, 1)
                nc.gpsimd.memset(ones[:, :], 1.0).then_inc(consts_set, 1)
                nc.gpsimd.memset(sq_acc[:, :], 0.0).then_inc(sq_made, HG)
                pool.wait_ge(consts_set, 2)
                for t in range(TILES):
                    pool.wait_ge(var_ready, t + 1)
                    nc.gpsimd.tensor_scalar(rstd[:, t % 2:t % 2 + 1], mv[:, t % 2, 1:2], EPS, None,
                                            ALU.add).then_inc(eps_added, 1)
                    pool.wait_ge(eps_added, t + 1)
                    nc.gpsimd.tensor_tensor(rstd[:, t % 2:t % 2 + 1], rstd[:, t % 2:t % 2 + 1], minus_half[:, :],
                                            ALU.pow).then_inc(rstd_ready, 1)
                pool.wait_ge(xn_ready, TILES)
                nc.gpsimd.memset(attn_acc[:, :, :], 0.0).then_inc(out_added, TT)

                def squares(g, tb, first=False):
                    for h in range(HG):
                        n = g * (TB * HG) + (tb * HG + h)
                        pool.wait_ge(attn_ready, n + 1)
                        pool.wait_ge(sq_made, n + HG)
                        if not (first and tb == 0 and h == 0):
                            pool.wait_ge(sq_added, n)
                        nc.gpsimd.tensor_tensor(sq[:, :], attn[:, h], attn[:, h], ALU.mult).then_inc(sq_made, 1)
                        pool.wait_ge(sq_made, n + HG + 1)
                        acc = sq_acc[:, tb * BT:(tb + 1) * BT]
                        nc.gpsimd.tensor_tensor(acc, acc, sq[:, :], ALU.add).then_inc(sq_added, 1)

                for tb in range(TB):
                    squares(0, tb, True)
                with pool.Fori(1, GROUPS) as g:
                    for tb in range(TB):
                        squares(g, tb)

            @block.scalar
            def _(act):
                def cut_hi(g, w):
                    ab, nth, per = ((0, (0, 0, 1, 0, 2)[w], 3) if w in (wq, wv, wo) else (1, (w - wk) // 2, 2))
                    act.wait_ge(raw_landed[ab], g * (16 * per) + 16 * (nth + 1))
                    if w == wo:
                        for h in range(HG):
                            i = nc.scalar.activation(w_hi[:, w, h * D:(h + 1) * D], raw[:, ab, h * D:(h + 1) * D],
                                                     ACT.Copy, scale=normw[:, bass.ds(g * HG + h, 1)])
                        i.then_inc(hi_cut, 1)
                    else:
                        nc.scalar.activation(w_hi[:, w], raw[:, ab], ACT.Copy).then_inc(hi_cut, 1)

                def sigmoids_qk(u):
                    for j in range(2 * HG):
                        act.wait_ge(qk_mm, u * (2 * HG) + (j + 1))
                        nc.scalar.activation(qk[:, j // HG, j % HG], bank[:, j], ACT.Sigmoid).then_inc(qk_sig, 1)

                def step(g, tb, last=False):
                    u = g * TB + tb
                    if tb == TB - 1 and not last:
                        act.wait_ge(v_mm, u * 2 + 1)
                        cut_hi(g + 1, wq)
                        cut_hi(g + 1, wk)
                    for j in range(2):
                        act.wait_ge(v_mm, u * 2 + (j + 1))
                        nc.scalar.activation(v[:, 2 * j:2 * j + 2], bank[:, j].rearrange("p (t n) -> p t n", t=2),
                                             ACT.Sigmoid).then_inc(v_sig, 1)
                    if tb == 0:
                        cut_hi(g, wo)
                    if tb == TB - 1 and not last:
                        cut_hi(g + 1, wv)
                    for h in range(HG):
                        act.wait_ge(g_mm, u * HG + (h + 1))
                        nc.scalar.activation(gate[:, h], bank[:, 4 + h], ACT.Sigmoid).then_inc(gate_ready, 1)
                    for h in range(HG):
                        act.wait_ge(pv_mm, u * HG + (h + 1))
                        act.wait_ge(sq_made, u * HG + (h + 1))
                        nc.scalar.activation(attn[:, h], bank[:, 6 + h], ACT.Copy).then_inc(attn_ready, 1)
                    if tb == TB - 1 and not last:
                        cut_hi(g + 1, wg)
                    for h in range(HG):
                        act.wait_ge(y_made, u * HG + (h + 1))
                        nc.scalar.activation(y_hi[:, h], gate[:, h], ACT.Copy).then_inc(y_hi_ready, 1)
                    if not (last and tb == TB - 1):
                        sigmoids_qk(u + 1)

                for t in range(TILES):
                    act.wait_ge(xn_turned, t + 1)
                    nc.scalar.activation(xn_hi[:, :, t * P:(t + 1) * P],
                                         bank[:, t % 4].rearrange("p (c n) -> p c n", c=CH),
                                         ACT.Copy).then_inc(xn_hi_ready, 1)
                    if t < 4:
                        cut_hi(0, t)
                act.wait_ge(normw_landed, 16)
                sigmoids_qk(0)
                with act.Fori(0, GROUPS - 1) as g:
                    for tb in range(TB):
                        step(g, tb)
                for tb in range(TB):
                    step(GROUPS - 1, tb, True)

            @block.vector
            def _(dve):
                def cut_lo(g, w):
                    ab = 0 if w in (wq, wv, wo) else 1
                    dve.wait_ge(hi_cut, g * 5 + (w + 1))
                    if w == wo:
                        for h in range(HG):
                            i = nc.vector.scalar_tensor_tensor(
                                out=w_lo[:, w, h * D:(h + 1) * D], in0=raw[:, ab, h * D:(h + 1) * D],
                                scalar=normw[:, bass.ds(g * HG + h, 1)],
                                in1=w_hi[:, w, h * D:(h + 1) * D].bitcast(F32), op0=ALU.mult, op1=ALU.subtract)
                    else:
                        i = nc.vector.tensor_tensor(w_lo[:, w], raw[:, ab], w_hi[:, w].bitcast(F32), ALU.subtract)
                    i.then_inc(w_ready, 1)

                def silus_qk(u):
                    for j in range(2 * HG):
                        dve.wait_ge(qk_sig, u * (2 * HG) + (j + 1))
                        o = qk[:, j // HG, j % HG]
                        nc.vector.tensor_tensor(o, bank[:, j], o, ALU.mult).then_inc(qk_ready, 1)

                def step(g, tb, last=False):
                    u = g * TB + tb
                    if tb == TB - 1 and not last:
                        cut_lo(g + 1, wq)
                        cut_lo(g + 1, wk)
                    for j in range(2):
                        dve.wait_ge(v_sig, u * 2 + (j + 1))
                        o = v[:, 2 * j:2 * j + 2]
                        nc.vector.tensor_tensor(o, bank[:, j].rearrange("p (t n) -> p t n", t=2), o,
                                                ALU.mult).then_inc(v_ready, 1)
                    if tb == 0:
                        cut_lo(g, wo)
                        dve.wait_ge(decay_landed, g * 16 + 16)
                    for h in range(HG):
                        dve.wait_ge(s_mm, u * HG + (h + 1))
                        nc.vector.tensor_tensor(scores[:, h].rearrange("p (t n) -> p t n", t=TT),
                                                bank[:, 2 + h].rearrange("p (t n) -> p t n", t=TT),
                                                decays[:, h:h + 1].broadcast_to([P, TT, P]),
                                                ALU.mult).then_inc(scores_ready, 1)
                    if tb == TB - 1 and not last:
                        cut_lo(g + 1, wv)
                    for h in range(HG):
                        dve.wait_ge(attn_ready, u * HG + (h + 1))
                        nc.vector.tensor_tensor(gate[:, h], gate[:, h], attn[:, h], ALU.mult).then_inc(y_made, 1)
                    for h in range(HG):
                        dve.wait_ge(y_hi_ready, u * HG + (h + 1))
                        nc.vector.tensor_tensor(y_lo[:, h], gate[:, h], y_hi[:, h].bitcast(F32),
                                                ALU.subtract).then_inc(y_ready, 1)
                    if tb == TB - 1 and not last:
                        cut_lo(g + 1, wg)
                    if not (last and tb == TB - 1):
                        silus_qk(u + 1)
                    for i in range(TT):
                        dve.wait_ge(out_mm, u * TT + (i + 1))
                        acc = attn_acc[:, tb * TT + i]
                        nc.vector.tensor_tensor(acc, acc, bank[:, 4 + i], ALU.add).then_inc(out_added, 1)

                def lo(t):
                    dve.wait_ge(xn_hi_ready, t + 1)
                    s = slice(t * P, (t + 1) * P)
                    nc.vector.tensor_tensor(xn_lo[:, :, s], bank[:, t % 4].rearrange("p (c n) -> p c n", c=CH),
                                            xn_hi[:, :, s].bitcast(F32), ALU.subtract).then_inc(xn_lo_ready, 1)

                def statistics(t):
                    if t % TT == 0:
                        dve.wait_ge(x_landed[t // TT], 16)
                    nc.vector.bn_stats(stats[:, t % 2], attn_acc[:, t]).then_inc(stats_done, 1)
                    dve.wait_ge(stats_done, t + 1)
                    nc.vector.bn_aggr(mv[:, t % 2], stats[:, t % 2]).then_inc(var_ready, 1)

                statistics(0)
                for t in range(TILES):
                    if t + 1 < TILES:
                        statistics(t + 1)
                    dve.wait_ge(rstd_ready, t + 1)
                    if t >= 2:
                        dve.wait_ge(xn_turned, t - 1)
                    nc.vector.tensor_scalar(xn[:, t % 2], attn_acc[:, t], mv[:, t % 2, 0:1],
                                            rstd[:, t % 2:t % 2 + 1], ALU.subtract, ALU.mult).then_inc(xn_ready, 1)
                    if t >= 1:
                        lo(t - 1)
                    if 1 <= t < 5:
                        cut_lo(0, t - 1)
                lo(TILES - 1)
                silus_qk(0)
                with dve.Fori(0, GROUPS - 1) as g:
                    for tb in range(TB):
                        step(g, tb)
                for tb in range(TB):
                    step(GROUPS - 1, tb, True)

            @block.tensor
            def _(pe):
                def weights(half, w, c, h):
                    return half[:, w, c * HG * HD + h * HD:c * HG * HD + (h + 1) * HD]

                def project(dst, w, h, tb, done):
                    s = slice(tb * BT, (tb + 1) * BT)
                    for c in range(CH):
                        hi = weights(w_hi, w, c, h)
                        nc.tensor.matmul(dst, hi, xn_hi[:, c, s], start=(c == 0), stop=False)
                        nc.tensor.matmul(dst, hi, xn_lo[:, c, s], start=False, stop=False)
                        i = nc.tensor.matmul(dst, weights(w_lo, w, c, h), xn_hi[:, c, s],
                                             start=False, stop=(c == CH - 1))
                    i.then_inc(done, 1)

                def project_qk(g, tb):
                    for j in range(2 * HG):
                        if tb == 0 and j % HG == 0:
                            pe.wait_ge(w_ready, g * 5 + (j // HG + 1))
                        project(bank[:, j], j // HG, j % HG, tb, qk_mm)

                def step(g, tb, last=False):
                    u = g * TB + tb
                    pe.wait_ge(qk_ready, u * (2 * HG) + 2)
                    if tb == 0:
                        pe.wait_ge(w_ready, g * 5 + wv + 1)
                    for i in range(TT):
                        dst = bank[:, i // 2, (i % 2) * HG * HD:(i % 2 + 1) * HG * HD]
                        s = slice(tb * BT + i * P, tb * BT + (i + 1) * P)
                        for c in range(CH):
                            m = slice(c * HG * HD, (c + 1) * HG * HD)
                            nc.tensor.matmul(dst, xn_hi[:, c, s], w_hi[:, wv, m], start=(c == 0), stop=False)
                            nc.tensor.matmul(dst, xn_hi[:, c, s], w_lo[:, wv, m], start=False, stop=False)
                            k = nc.tensor.matmul(dst, xn_lo[:, c, s], w_hi[:, wv, m], start=False, stop=(c == CH - 1))
                        if i % 2:
                            k.then_inc(v_mm, 1)
                    pe.wait_ge(qk_ready, u * (2 * HG) + 2 * HG)
                    for h in range(HG):
                        for i in range(TT):
                            s = slice(i * P, (i + 1) * P)
                            k = nc.tensor.matmul(bank[:, 2 + h, s], qk[:, 1, h, s], qk[:, 0, h, s],
                                                 start=True, stop=True)
                        k.then_inc(s_mm, 1)
                    if tb == 0:
                        pe.wait_ge(w_ready, g * 5 + wg + 1)
                    for h in range(HG):
                        if h == 0:
                            pe.wait_ge(out_added, u * TT + 2)
                        project(bank[:, 4 + h], wg, h, tb, g_mm)
                    pe.wait_ge(v_ready, u * 2 + 2)
                    pe.wait_ge(out_added, u * TT + TT)
                    for h in range(HG):
                        pe.wait_ge(scores_ready, u * HG + (h + 1))
                        for i in range(TT):
                            s = slice(i * P, (i + 1) * P)
                            k = nc.tensor.matmul(bank[:, 6 + h, s], v[:, i, h * HD:(h + 1) * HD], scores[:, h, s],
                                                 start=True, stop=True)
                        k.then_inc(pv_mm, 1)
                    if not (last and tb == TB - 1):
                        project_qk(g if tb < TB - 1 else g + 1, (tb + 1) % TB)
                    if tb == 0:
                        pe.wait_ge(w_ready, g * 5 + wo + 1)
                    pe.wait_ge(y_ready, u * HG + HG)
                    for i in range(TT):
                        s = slice(i * P, (i + 1) * P)
                        for h in range(HG):
                            m = slice(h * D, (h + 1) * D)
                            nc.tensor.matmul(bank[:, 4 + i], y_hi[:, h, s], w_hi[:, wo, m], start=(h == 0), stop=False)
                            nc.tensor.matmul(bank[:, 4 + i], y_hi[:, h, s], w_lo[:, wo, m], start=False, stop=False)
                            k = nc.tensor.matmul(bank[:, 4 + i], y_lo[:, h, s], w_hi[:, wo, m],
                                                 start=False, stop=(h == HG - 1))
                        k.then_inc(out_mm, 1)

                pe.wait_ge(const_landed, 16)
                for t in range(TILES):
                    pe.wait_ge(xn_ready, t + 1)
                    if t >= 4:
                        pe.wait_ge(xn_lo_ready, t - 3)
                    for c in range(CH):
                        s = slice(c * P, (c + 1) * P)
                        k = nc.tensor.transpose(bank[:, t % 4, s], xn[:, t % 2, s], ident[:, :])
                    k.then_inc(xn_turned, 1)
                pe.wait_ge(xn_lo_ready, TILES)
                project_qk(0, 0)
                with pe.Fori(0, GROUPS - 1) as g:
                    for tb in range(TB):
                        step(g, tb)
                for tb in range(TB):
                    step(GROUPS - 1, tb, True)


def cross_and_ffn(nc, sb, sem, bank, x1, sq_acc, ident, ones, x, ctx_in, wq_in, wk_in, wv_in, bq_in, bk_in, bv_in,
                  eye_in, out):
    with ExitStack() as own:
        xr = sb(own, "xr", [P, TILES, D])
        ms = sb(own, "ms", [P, TILES])
        rrms = sb(own, "rrms", [P, TILES])
        minus_half = sb(own, "minus_half2", [P, TILES])
        ctx = sb(own, "ctx", [P, 2, D])
        ctx_parts = sb(own, "ctx_parts", [P, 2, D], F32R)
        wqk = sb(own, "wqk", [P, 2, P])
        wqk_hi = sb(own, "wqk_hi", [P, 2, P], F32R)
        wqk_lo = sb(own, "wqk_lo", [P, 2, P], F32R)
        bqk = sb(own, "bqk", [P, 2])
        wv = sb(own, "wv", [P, P])
        bv = sb(own, "bv", [P, P])
        q_parts = sb(own, "q_parts", [P, D], F32R)
        k_hi = sb(own, "k_hi", [P, D], F32R)
        k_lo = sb(own, "k_lo", [P, D], F32R)
        minus_max = sb(own, "minus_max", [P, 2, CH])
        row_sum = sb(own, "row_sum", [P, 2, CH])
        row_inv = sb(own, "row_inv", [P, 2, CH])
        prob = sb(own, "prob", [P, 2, CH, D])
        probT_hi = sb(own, "probT_hi", [P, 2, D], F32R)
        probT_lo = sb(own, "probT_lo", [P, 2, D], F32R)
        xn2 = sb(own, "xn2", [P, D])
        v32 = sb(own, "v32", [P, CH, 2, SEQ])
        v_hi = sb(own, "v_hi", [P, CH, 2, P], F32R)
        v_lo = sb(own, "v_lo", [P, CH, 2, P], F32R)
        xn3 = sb(own, "xn3", [P, D])
        xn3_hi = sb(own, "xn3_hi", [P, CH, P], F32R)
        xn3_lo = sb(own, "xn3_lo", [P, CH, P], F32R)
        eye = sb(own, "eye", [P, CH, D])
        eye_hi = sb(own, "eye_hi", [P, CH, D], F32R)
        eye_lo = sb(own, "eye_lo", [P, CH, D], F32R)
        stats = sb(own, "stats2", [P, 2, 6])
        mv = sb(own, "mv2", [P, 2, 2])
        rstd = sb(own, "rstd2", [P, 2])

        names = """summed ms_ready rrms_ready x1_ready consts_landed eye_landed consts_set wqk_hi_cut wqk_cut
            eye_hi_cut eye_cut ctx_hi_ready ctx_ready qk_mm qk_hi_ready qk_ready r_mm max_ready exp_ready inv_ready
            prob_ready turned probT_hi_ready probT_ready pv_mm x2_ready ln2_stats ln2_var ln2_eps ln2_rstd xn2_ready
            v_mm v_made v_hi_ready v_ready ln3_stats ln3_var ln3_eps ln3_rstd xn3_ready xn3_turned xn3_hi_ready
            xn3T_ready ffn_mm out_ready stored""".split()
        S = {n: sem("b_" + n) for n in names}
        passed = sem("passed")
        x_back = [sem(f"x_back{i}") for i in range(TB)]
        ctx_landed = [sem(f"ctx_landed{i}") for i in range(2)]
        x_t = x.rearrange("b s d -> (b s) d").rearrange("(k t p) d -> k p t d", t=TT, p=P)
        out_t = out.rearrange("b s d -> (b s) d").rearrange("(t p) d -> t p d", p=P)
        PAIRS = TILES
        Q, K, OUT, MISC = 4, 5, 6, 7

        with nc.Block() as block:

            @block.sync
            def _(sp):
                def load_ctx(b, i):
                    for half in range(2):
                        sp.dma_start(ctx[half * SEQ:(half + 1) * SEQ, i], ctx_in[b]).then_inc(ctx_landed[i], 16)

                for i in range(2):
                    load_ctx(i, i)
                for dst, src in ((wqk[:, 0], wq_in), (wqk[:, 1], wk_in), (bqk[:, 0:1], bq_in), (bqk[:, 1:2], bk_in),
                                 (wv[:, :], wv_in), (bv[:, :], bv_in)):
                    sp.dma_start(dst, src).then_inc(S["consts_landed"], 16)
                for k in range(TB):
                    sp.dma_start(xr[:, k * TT:(k + 1) * TT], x_t[k]).then_inc(x_back[k], 16)
                sp.dma_start(eye[:, :, :], eye_in).then_inc(S["eye_landed"], 16)

                def store(t):
                    sp.wait_ge(S["out_ready"], t + 1)
                    sp.dma_start(out_t[t], x1[:, t]).then_inc(S["stored"], 16)

                def pair(t, first=False):
                    for i in range(2):
                        sp.wait_ge(S["ctx_ready"], t * 2 + (i + 1))
                        load_ctx(t * 2 + (2 + i), i)
                    if not first:
                        store(t - 1)

                pair(0, True)
                with sp.Fori(1, PAIRS - 1) as t:
                    pair(t)
                store(PAIRS - 2)
                store(PAIRS - 1)
                sp.wait_ge(S["stored"], 16 * PAIRS)

            @block.gpsimd
            def _(pool):
                nc.gpsimd.memset(minus_half[:, :], -0.5).then_inc(S["consts_set"], 1)
                nc.gpsimd.memset(v_hi[:, :, :, :].bitcast(F32), 0.0).then_inc(S["consts_set"], 1)
                nc.gpsimd.memset(v_lo[:, :, :, :].bitcast(F32), 0.0).then_inc(S["consts_set"], 1)
                pool.wait_ge(S["consts_set"], 3)

                def ctx_lo(b, i):
                    pool.wait_ge(S["ctx_hi_ready"], b + 1)
                    lo = slice(SEQ, P)
                    nc.gpsimd.tensor_tensor(ctx_parts[lo, i], ctx[lo, i], ctx_parts[lo, i].bitcast(F32),
                                            ALU.subtract).then_inc(S["ctx_ready"], 1)
                    pool.wait_ge(S["ctx_ready"], b + 1)

                def inv_root(n, k, t):
                    wait_apart(pool, S[f"ln{n}_var"], t + 1, passed)
                    nc.gpsimd.tensor_scalar(rstd[:, k:k + 1], mv[:, k, 1:2], EPS, None,
                                            ALU.add).then_inc(S[f"ln{n}_eps"], 1)
                    pool.wait_ge(S[f"ln{n}_eps"], t + 1)
                    nc.gpsimd.tensor_tensor(rstd[:, k:k + 1], rstd[:, k:k + 1], minus_half[:, 0:1],
                                            ALU.pow).then_inc(S[f"ln{n}_rstd"], 1)

                def normalise(b, i):
                    for j in range(CH):
                        wait_apart(pool, S["inv_ready"], b * CH + (j + 1), passed)
                        nc.gpsimd.tensor_scalar(prob[:, i, j], prob[:, i, j], row_inv[:, i, j:j + 1], None,
                                                ALU.mult).then_inc(S["prob_ready"], 1)

                def v_rest(t):
                    pool.wait_ge(S["v_hi_ready"], t + 1)
                    nc.gpsimd.tensor_tensor(v_lo[:, :, :, 0:SEQ], v32[:, :, :, :],
                                            v_hi[:, :, :, 0:SEQ].bitcast(F32), ALU.subtract).then_inc(S["v_ready"], 1)

                def pair(t, first=False, last=False):
                    for i in range(2):
                        if not last:
                            pool.wait_ge(*((S["ln2_rstd"], t + 2) if i else (S["v_ready"], t + 1)))
                            ctx_lo(t * 2 + (i + 2), i)
                        if i == 0 and not first:
                            inv_root(3, 1, t - 1)
                        if not (last and i == 1):
                            normalise(t * 2 + (i + 1), 1 - i)
                        if i == 0 and not last:
                            inv_root(2, 0, t + 1)
                    if not last:
                        v_rest(t + 1)

                ctx_lo(0, 0)
                ctx_lo(1, 1)
                pool.wait_ge(S["ms_ready"], 1)
                nc.gpsimd.tensor_tensor(rrms[:, :], ms[:, :], minus_half[:, :], ALU.pow).then_inc(S["rrms_ready"], 1)
                inv_root(2, 0, 0)
                normalise(0, 0)
                v_rest(0)
                pair(0, first=True)
                with pool.Fori(1, PAIRS - 1) as t:
                    pair(t)
                pair(PAIRS - 1, last=True)
                inv_root(3, 1, PAIRS - 1)

            @block.scalar
            def _(act):
                def ctx_hi(b, i, nth):
                    act.wait_ge(ctx_landed[i], nth * 32)
                    nc.scalar.activation(ctx_parts[:, i], ctx[:, i], ACT.Copy).then_inc(S["ctx_hi_ready"], 1)

                def qk_hi(b):
                    for j, dst in enumerate((q_parts, k_hi)):
                        act.wait_ge(S["qk_mm"], b * 2 + (j + 1))
                        nc.scalar.activation(dst[:, :], bank[:, Q + j], ACT.Identity,
                                             bias=bqk[:, j:j + 1]).then_inc(S["qk_hi_ready"], 1)

                def exps(b, i, j):
                    act.wait_ge(S["max_ready"], b * CH + (j + 1))
                    nc.scalar.activation(prob[:, i, j], bank[:, j % 2], ACT.Exp, bias=minus_max[:, i, j:j + 1],
                                         accum_out=row_sum[:, i, j:j + 1]).then_inc(S["exp_ready"], 1)

                def turned_hi(b, j):
                    act.wait_ge(S["turned"], b * CH + (j + 1))
                    nc.scalar.activation(probT_hi[:, j % 2], bank[:, 2 + j % 2], ACT.Copy)\
                        .then_inc(S["probT_hi_ready"], 1)

                def v_high(t):
                    act.wait_ge(S["v_made"], t + 1)
                    nc.scalar.activation(v_hi[:, :, :, 0:SEQ], v32[:, :, :, :], ACT.Copy).then_inc(S["v_hi_ready"], 1)

                def xn3_high(t):
                    act.wait_ge(S["xn3_turned"], t + 1)
                    nc.scalar.activation(xn3_hi[:, :, :], bank[:, MISC].rearrange("p (c n) -> p c n", c=CH),
                                         ACT.Copy).then_inc(S["xn3_hi_ready"], 1)

                def pair(t, first=False, last=False):
                    for i in range(2):
                        b = t * 2 + i
                        more = not (last and i == 1)
                        if not last:
                            ctx_hi(b + 2, i, t + 2)
                        if i == 1 and not first:
                            xn3_high(t - 1)
                        for j in range(CH):
                            if more:
                                exps(b + 1, 1 - i, j)
                            turned_hi(b, j)
                        if not last:
                            qk_hi(b + 2)
                    if not last:
                        v_high(t + 1)

                act.wait_ge(S["consts_landed"], 16 * 6)
                nc.scalar.activation(wqk_hi[:, :, :], wqk[:, :, :], ACT.Copy).then_inc(S["wqk_hi_cut"], 1)
                ctx_hi(0, 0, 1)
                ctx_hi(1, 1, 1)
                qk_hi(0)
                for j in range(CH):
                    exps(0, 0, j)
                qk_hi(1)
                act.wait_ge(S["consts_set"], 3)
                v_high(0)
                act.wait_ge(S["eye_landed"], 16)
                nc.scalar.activation(eye_hi[:, :, :], eye[:, :, :], ACT.Copy).then_inc(S["eye_hi_cut"], 1)
                pair(0, first=True)
                with act.Fori(1, PAIRS - 1) as t:
                    pair(t)
                pair(PAIRS - 1, last=True)
                xn3_high(PAIRS - 1)

            @block.vector
            def _(dve):
                def qk_lo(b):
                    lo = slice(SEQ, P)
                    dve.wait_ge(S["qk_hi_ready"], b * 2 + 1)
                    nc.vector.scalar_tensor_tensor(out=q_parts[lo, :], in0=bank[lo, Q], scalar=bqk[lo, 0:1],
                                                   in1=q_parts[lo, :].bitcast(F32), op0=ALU.add,
                                                   op1=ALU.subtract).then_inc(S["qk_ready"], 1)
                    dve.wait_ge(S["qk_hi_ready"], b * 2 + 2)
                    nc.vector.scalar_tensor_tensor(out=k_lo[:, :], in0=bank[:, K], scalar=bqk[:, 1:2],
                                                   in1=k_hi[:, :].bitcast(F32), op0=ALU.add,
                                                   op1=ALU.subtract).then_inc(S["qk_ready"], 1)

                def row_max(b, i, j):
                    dve.wait_ge(S["r_mm"], b * CH + (j + 1))
                    nc.vector.tensor_reduce(minus_max[:, i, j:j + 1], bank[:, j % 2], AX.X, ALU.max,
                                            negate=True).then_inc(S["max_ready"], 1)

                def inverse(b, i, j):
                    dve.wait_ge(S["exp_ready"], b * CH + (j + 1))
                    nc.vector.reciprocal(row_inv[:, i, j:j + 1], row_sum[:, i, j:j + 1]).then_inc(S["inv_ready"], 1)

                def turned_lo(b, j):
                    dve.wait_ge(S["probT_hi_ready"], b * CH + (j + 1))
                    nc.vector.tensor_tensor(probT_lo[:, j % 2], bank[:, 2 + j % 2], probT_hi[:, j % 2].bitcast(F32),
                                            ALU.subtract).then_inc(S["probT_ready"], 1)

                def make_x1(t):
                    nc.vector.scalar_tensor_tensor(out=x1[:, t], in0=x1[:, t], scalar=rrms[:, bass.ds(t, 1)],
                                                   in1=xr[:, t], op0=ALU.mult, op1=ALU.add)\
                        .then_inc(S["x1_ready"], 1)
                    wait_apart(dve, S["x1_ready"], t + 1, passed)

                def layernorm(n, k, t, dst):
                    nc.vector.bn_stats(stats[:, k], x1[:, t]).then_inc(S[f"ln{n}_stats"], 1)
                    wait_apart(dve, S[f"ln{n}_stats"], t + 1, passed)
                    nc.vector.bn_aggr(mv[:, k], stats[:, k]).then_inc(S[f"ln{n}_var"], 1)

                def normed(n, k, t, dst):
                    dve.wait_ge(S[f"ln{n}_rstd"], t + 1)
                    nc.vector.tensor_scalar(dst[:, :], x1[:, t], mv[:, k, 0:1], rstd[:, k:k + 1], ALU.subtract,
                                            ALU.mult).then_inc(S[f"xn{n}_ready"], 1)

                def make_v(t):
                    dve.wait_ge(S["v_mm"], t + 1)
                    nc.vector.tensor_tensor(v32[:, :, :, :].rearrange("p c b o -> p c (b o)"),
                                            bank[:, MISC].rearrange("p (c n) -> p c n", c=CH),
                                            bv[:, :].rearrange("p (a n) -> p a n", a=1).broadcast_to([P, CH, P]),
                                            ALU.add).then_inc(S["v_made"], 1)

                def xn3_low(t):
                    dve.wait_ge(S["xn3_hi_ready"], t + 1)
                    nc.vector.tensor_tensor(xn3_lo[:, :, :], bank[:, MISC].rearrange("p (c n) -> p c n", c=CH),
                                            xn3_hi[:, :, :].bitcast(F32), ALU.subtract).then_inc(S["xn3T_ready"], 1)

                def add_cross(t):
                    dve.wait_ge(S["pv_mm"], t + 1)
                    nc.vector.tensor_tensor(x1[:, t], x1[:, t], bank[:, OUT], ALU.add).then_inc(S["x2_ready"], 1)
                    wait_apart(dve, S["x2_ready"], t + 1, passed)

                def add_ffn(t):
                    dve.wait_ge(S["ffn_mm"], t + 1)
                    nc.vector.tensor_tensor(x1[:, t], x1[:, t], bank[:, MISC], ALU.add).then_inc(S["out_ready"], 1)

                def pair(t, first=False, last=False):
                    for i in range(2):
                        b = t * 2 + i
                        more = not (last and i == 1)
                        if i == 0 and not first:
                            layernorm(3, 1, t - 1, xn3)
                        if i == 1 and not first:
                            xn3_low(t - 1)
                        for j in range(CH):
                            if more:
                                row_max(b + 1, 1 - i, j)
                            turned_lo(b, j)
                            if more and j:
                                inverse(b + 1, 1 - i, j - 1)
                            if i == 0 and j == 1 and not first:
                                normed(3, 1, t - 1, xn3)
                            if i == 0 and j == 2 and not last:
                                if first:
                                    dve.wait_ge(x_back[0], 16)
                                make_x1(t + 1)
                                layernorm(2, 0, t + 1, xn2)
                        if more:
                            inverse(b + 1, 1 - i, CH - 1)
                        if not last:
                            qk_lo(b + 2)
                        if i == 0 and not last:
                            normed(2, 0, t + 1, xn2)
                        if i == 1 and not first:
                            add_ffn(t - 1)
                    add_cross(t)
                    if not last:
                        make_v(t + 1)

                dve.wait_ge(S["wqk_hi_cut"], 1)
                nc.vector.tensor_tensor(wqk_lo[:, :, :], wqk[:, :, :], wqk_hi[:, :, :].bitcast(F32),
                                        ALU.subtract).then_inc(S["wqk_cut"], 1)
                dve.wait_ge(S["summed"], 1)
                nc.vector.tensor_scalar(ms[:, :], bank[:, MISC, 0:TILES], 1.0 / (HEADS * HD), EPS, ALU.mult,
                                        ALU.add).then_inc(S["ms_ready"], 1)
                qk_lo(0)
                for j in range(CH):
                    row_max(0, 0, j)
                    inverse(0, 0, j)
                qk_lo(1)
                dve.wait_ge(S["rrms_ready"], 1)
                for k in range(TB):
                    dve.wait_ge(x_back[k], 16)
                make_x1(0)
                layernorm(2, 0, 0, xn2)
                normed(2, 0, 0, xn2)
                make_v(0)
                dve.wait_ge(S["eye_hi_cut"], 1)
                nc.vector.tensor_tensor(eye_lo[:, :, :], eye[:, :, :], eye_hi[:, :, :].bitcast(F32),
                                        ALU.subtract).then_inc(S["eye_cut"], 1)
                pair(0, first=True)
                with dve.Fori(1, PAIRS - 1) as t:
                    pair(t)
                pair(PAIRS - 1, last=True)
                layernorm(3, 1, PAIRS - 1, xn3)
                normed(3, 1, PAIRS - 1, xn3)
                xn3_low(PAIRS - 1)
                add_ffn(PAIRS - 1)

            @block.tensor
            def _(pe):
                def project(b, i):
                    pe.wait_ge(S["ctx_ready"], b + 1)
                    for j in range(2):
                        nc.tensor.matmul(bank[:, Q + j], wqk_hi[:, j], ctx_parts[:, i], start=True, stop=False)
                        nc.tensor.matmul(bank[:, Q + j], wqk_lo[:, j], ctx_parts[:, i], start=False,
                                         stop=True).then_inc(S["qk_mm"], 1)

                def cross_scores(b, j, begun=True):
                    if begun:
                        pe.wait_ge(S["exp_ready"], b * CH + (j - 1))
                    if j == 0:
                        pe.wait_ge(S["qk_ready"], b * 2 + 2)
                    q = q_parts[:, j * P:(j + 1) * P]
                    nc.tensor.matmul(bank[:, j % 2], q, k_hi[:, :], start=True, stop=False)
                    nc.tensor.matmul(bank[:, j % 2], q, k_lo[:, :], start=False, stop=True).then_inc(S["r_mm"], 1)

                def turn(b, i, j):
                    if j == 0:
                        pe.wait_ge(S["prob_ready"], b * CH + CH)
                    for k in range(CH):
                        m = nc.tensor.transpose(bank[:, 2 + j % 2, k * P:(k + 1) * P],
                                                prob[:, i, k, j * P:(j + 1) * P], ident[:, :])
                    m.then_inc(S["turned"], 1)

                def weigh(b, i, j):
                    pe.wait_ge(S["probT_ready"], b * CH + (j + 1))
                    cols = slice(i * SEQ, i * SEQ + P)
                    vh = v_hi[:, j].rearrange("p b o -> p (b o)")[:, cols]
                    vl = v_lo[:, j].rearrange("p b o -> p (b o)")[:, cols]
                    nc.tensor.matmul(bank[:, OUT], vh, probT_hi[:, j % 2], start=(i == 0 and j == 0), stop=False)
                    nc.tensor.matmul(bank[:, OUT], vh, probT_lo[:, j % 2], start=False, stop=False)
                    m = nc.tensor.matmul(bank[:, OUT], vl, probT_hi[:, j % 2], start=False,
                                         stop=(i == 1 and j == CH - 1))
                    if i == 1 and j == CH - 1:
                        m.then_inc(S["pv_mm"], 1)

                def values(t, first=False):
                    pe.wait_ge(S["xn2_ready"], t + 1)
                    if not first:
                        pe.wait_ge(S["out_ready"], t - 1)
                    for c in range(CH):
                        m = nc.tensor.matmul(bank[:, MISC, c * P:(c + 1) * P], xn2[:, c * P:(c + 1) * P], wv[:, :],
                                             start=True, stop=True)
                    m.then_inc(S["v_mm"], 1)

                def turn_xn3(t):
                    pe.wait_ge(S["xn3_ready"], t + 1)
                    for c in range(CH):
                        s = slice(c * P, (c + 1) * P)
                        m = nc.tensor.transpose(bank[:, MISC, s], xn3[:, s], ident[:, :])
                    m.then_inc(S["xn3_turned"], 1)

                def ffn(t):
                    pe.wait_ge(S["xn3T_ready"], t + 1)
                    for c in range(CH):
                        nc.tensor.matmul(bank[:, MISC], xn3_hi[:, c], eye_hi[:, c], start=(c == 0), stop=False)
                        nc.tensor.matmul(bank[:, MISC], xn3_hi[:, c], eye_lo[:, c], start=False, stop=False)
                        m = nc.tensor.matmul(bank[:, MISC], xn3_lo[:, c], eye_hi[:, c], start=False,
                                             stop=(c == CH - 1))
                    m.then_inc(S["ffn_mm"], 1)

                def pair(t, first=False, last=False):
                    for i in range(2):
                        b = t * 2 + i
                        more = not (last and i == 1)
                        if i == 0:
                            pe.wait_ge(S["v_ready"], t + 1)
                            if not first:
                                pe.wait_ge(S["x2_ready"], t)
                        for j in range(CH):
                            if more:
                                cross_scores(b + 1, j)
                            turn(b, i, j)
                            if j:
                                weigh(b, i, j - 1)
                            if i == 1 and j == 2 and not first:
                                ffn(t - 1)
                        if not last:
                            project(b + 2, i)
                        weigh(b, i, CH - 1)
                        if i == 0 and not first:
                            turn_xn3(t - 1)
                    if not last:
                        values(t + 1, first)

                for t in range(TILES):
                    m = nc.tensor.matmul(bank[:, MISC, t:t + 1], sq_acc[:, t * P:(t + 1) * P], ones[:, 0:1],
                                         start=True, stop=True)
                m.then_inc(S["summed"], 1)
                pe.wait_ge(S["wqk_cut"], 1)
                project(0, 0)
                for j in range(CH):
                    cross_scores(0, j, j >= 2)
                project(1, 1)
                pe.wait_ge(S["ms_ready"], 1)
                values(0, True)
                pe.wait_ge(S["eye_cut"], 1)
                pair(0, first=True)
                with pe.Fori(1, PAIRS - 1) as t:
                    pair(t)
                pair(PAIRS - 1, last=True)
                turn_xn3(PAIRS - 1)
                ffn(PAIRS - 1)


def kernel(x, ctx_4096, L0_attn_qkv_w, L0_attn_out_w, L0_attn_gate_w, L0_attn_norm_w, L0_xattn_Wq, L0_xattn_bq,
           L0_xattn_Wk, L0_xattn_bk, L0_xattn_Wv, L0_xattn_bv, L0_ffn_identity):
    import concourse.bacc as bacc
    from concourse.bass_utils import run_bass_kernel_spmd

    def rows(w):
        w = w.reshape(GROUPS, HG, HD, CH, P).transpose(0, 4, 3, 1, 2)
        return np.ascontiguousarray(w.reshape(GROUPS, P, CH * HG * HD))

    qkv = np.asarray(L0_attn_qkv_w).reshape(HEADS, 3, HD, D)
    arrays = {
        "x": np.asarray(x),
        "ctx_in": np.asarray(ctx_4096),
        "w_qkv": np.ascontiguousarray(np.stack([rows(qkv[:, i]) for i in range(3)], axis=1)),
        "w_gate": rows(np.asarray(L0_attn_gate_w)),
        "w_out": np.ascontiguousarray(np.asarray(L0_attn_out_w).reshape(D, GROUPS, HG, HD).transpose(1, 3, 2, 0)
                                      .reshape(GROUPS, HD, HG * D)),
        "norm_w": np.ascontiguousarray(np.asarray(L0_attn_norm_w).reshape(HEADS, HD).T),
        "decay": decay_table(),
        "ident_in": np.eye(P, dtype=np.float32),
    }
    twice = lambda w: np.tile(np.asarray(w).T, (2, 2))
    column = lambda v: np.ascontiguousarray(np.tile(np.asarray(v), 2)[:, None])
    wv = np.zeros((P, P), np.float32)
    wv[:SEQ, :SEQ] = wv[SEQ:, SEQ:] = np.asarray(L0_xattn_Wv).T
    arrays |= {
        "wq_in": twice(L0_xattn_Wq), "wk_in": twice(L0_xattn_Wk), "wv_in": wv,
        "bq_in": column(L0_xattn_bq), "bk_in": column(L0_xattn_bk),
        "bv_in": np.tile(np.asarray(L0_xattn_bv), (P, 2)),
        "eye_in": np.ascontiguousarray(np.asarray(L0_ffn_identity).T.reshape(CH, P, D).transpose(1, 0, 2)),
    }
    nc = bacc.Bacc("TRN2", target_bir_lowering=False, num_devices=1)
    args = {n: nc.dram_tensor(n, a.shape, mybir.dt.from_np(a.dtype), kind="ExternalInput").ap()
            for n, a in arrays.items()}
    out = nc.dram_tensor("out", (B, SEQ, D), F32, kind="ExternalOutput").ap()
    decoder_layer(nc, **args, out=out)
    r = run_bass_kernel_spmd(nc, [arrays], core_ids=[0])
    return r.results[0]["out"]
```

```python
from contextlib import ExitStack

import numpy as np

import concourse.bass as bass
from concourse import mybir
from concourse.alu_op_type import AluOpType as ALU

ACT = mybir.ActivationFunctionType
AX = mybir.AxisListType
F32 = mybir.dt.float32
F32R = mybir.dt.float32r

P = 128
B, SEQ, D = 32, 64, 512
TOKENS = B * SEQ
TILES = TOKENS // P
CH = D // P
HEADS, HD = 32, 128
HG = 2
GROUPS = HEADS // HG
TB = 4
BT = TOKENS // TB
TT = BT // P
EPS = 1e-5
LAYER_IDX, N_LAYERS = 1, 32


def decay_table():
    f = np.float32
    base = f(1.0 / 2.0 ** (8.0 / HEADS))
    factor = f(1.0 - LAYER_IDX / (N_LAYERS - 1 + 1e-5) + 1e-5)
    slope = (base ** (np.arange(HEADS, dtype=f) + f(1.0)) * factor).astype(np.float64)
    m = np.arange(P)[:, None, None]
    n = np.arange(P)[None, None, :]
    seen = (n >= m) & (n // SEQ == m // SEQ)
    return np.where(seen, np.exp(-slope[None, :, None] * np.maximum(n - m, 0)), 0.0).astype(f)


def decoder_layer(nc, x, ctx_in, w_qkv, w_gate, w_out, norm_w, decay, ident_in, wq_in, wk_in, wv_in, bq_in, bk_in,
                  bv_in, eye_in, out):
    with ExitStack() as both:
        def sb(stack, name, shape, dt=F32):
            return stack.enter_context(nc.sbuf_tensor(name, shape, dt))

        def sem(name):
            return both.enter_context(nc.semaphore(name))

        bank = both.enter_context(nc.psum_tensor("bank", [P, 8, 512], F32))
        attn_acc = sb(both, "attn_acc", [P, TILES, D])
        sq_acc = sb(both, "sq_acc", [P, TOKENS])
        ident = sb(both, "ident", [P, P])
        ones = sb(both, "ones", [P, 2])

        attention(nc, sb, sem, bank, attn_acc, sq_acc, ident, ones,
                  x, w_qkv, w_gate, w_out, norm_w, decay, ident_in)
        cross_and_ffn(nc, sb, sem, bank, attn_acc, sq_acc, ident, ones, x, ctx_in, wq_in, wk_in, wv_in, bq_in, bk_in,
                      bv_in, eye_in, out)


def wait_apart(eng, sem, value, passed):
    eng.wait_ge(sem, value)
    eng.sem_inc(passed, 1)


def attention(nc, sb, sem, bank, attn_acc, sq_acc, ident, ones, x, w_qkv, w_gate, w_out, norm_w, decay, ident_in):
    with ExitStack() as own:
        xn_hi = sb(own, "xn_hi", [P, CH, TOKENS], F32R)
        xn_lo = sb(own, "xn_lo", [P, CH, TOKENS], F32R)
        w_hi = sb(own, "w_hi", [P, 5, CH * HG * HD], F32R)
        w_lo = sb(own, "w_lo", [P, 5, CH * HG * HD], F32R)
        raw = sb(own, "raw", [P, 2, CH * HG * HD])
        decays = sb(own, "decays", [P, HG, P])
        normw = sb(own, "normw", [P, HEADS])
        qk = sb(own, "qk", [P, 2, HG, BT])
        v = sb(own, "v", [P, TT, HG * HD])
        scores = sb(own, "scores", [P, HG, BT])
        gate = sb(own, "gate", [P, HG, BT])
        attn = sb(own, "attn", [P, HG, BT])
        y_hi = sb(own, "y_hi", [P, HG, BT], F32R)
        y_lo = sb(own, "y_lo", [P, HG, BT], F32R)
        sq = sb(own, "sq", [P, BT])
        xn = sb(own, "xn", [P, 2, D])
        stats = sb(own, "stats", [P, 2, 6])
        mv = sb(own, "mv", [P, 2, 2])
        rstd = sb(own, "rstd", [P, 2])
        minus_half = sb(own, "minus_half", [P, 1])

        wq, wk, wv, wg, wo = range(5)

        x_landed = [sem(f"x_landed{i}") for i in range(TB)]
        const_landed = sem("const_landed")
        normw_landed = sem("normw_landed")
        consts_set = sem("consts_set")
        decay_landed = sem("decay_landed")
        raw_landed = [sem("raw_landed_a"), sem("raw_landed_b")]
        hi_cut = sem("hi_cut")
        w_ready = sem("w_ready")
        stats_done = sem("stats_done")
        var_ready = sem("var_ready")
        eps_added = sem("eps_added")
        rstd_ready = sem("rstd_ready")
        xn_ready = sem("xn_ready")
        xn_turned = sem("xn_turned")
        xn_hi_ready = sem("xn_hi_ready")
        xn_lo_ready = sem("xn_lo_ready")
        v_mm, s_mm, g_mm, pv_mm, qk_mm, out_mm = (sem(n) for n in ("v_mm", "s_mm", "g_mm", "pv_mm", "qk_mm", "out_mm"))
        v_sig, qk_sig, gate_ready, attn_ready = (sem(n) for n in ("v_sig", "qk_sig", "gate_ready", "attn_ready"))
        v_ready, qk_ready, scores_ready = (sem(n) for n in ("v_ready", "qk_ready", "scores_ready"))
        y_made, y_hi_ready, y_ready = (sem(n) for n in ("y_made", "y_hi_ready", "y_ready"))
        out_added = sem("out_added")
        sq_made, sq_added = sem("sq_made"), sem("sq_added")

        x_t = x.rearrange("b s d -> (b s) d").rearrange("(k t p) d -> k p t d", t=TT, p=P)

        with nc.Block() as block:

            @block.sync
            def _(sp):
                sp.dma_start(ident[:, :], ident_in).then_inc(const_landed, 16)
                for k in range(TB):
                    sp.dma_start(attn_acc[:, k * TT:(k + 1) * TT], x_t[k]).then_inc(x_landed[k], 16)
                sp.dma_start(raw[:, 0], w_qkv[0, 0]).then_inc(raw_landed[0], 16)
                sp.dma_start(raw[:, 1], w_qkv[0, 1]).then_inc(raw_landed[1], 16)
                sp.dma_start(normw[:, :], norm_w).then_inc(normw_landed, 16)
                sp.dma_start(decays[:, :, :], decay[:, 0:HG, :]).then_inc(decay_landed, 16)
                def rest_of_group(g):
                    sp.wait_ge(w_ready, g * 5 + (wq + 1))
                    sp.dma_start(raw[:, 0], w_qkv[g, 2]).then_inc(raw_landed[0], 16)
                    sp.wait_ge(w_ready, g * 5 + (wk + 1))
                    sp.dma_start(raw[:, 1], w_gate[g]).then_inc(raw_landed[1], 16)
                    sp.wait_ge(w_ready, g * 5 + (wv + 1))
                    sp.dma_start(raw[:, 0], w_out[g]).then_inc(raw_landed[0], 16)

                with nc.Fori(0, GROUPS - 1, engines=[sp.engine], hint_back_edge=True) as g:
                    rest_of_group(g)
                    sp.wait_ge(w_ready, g * 5 + (wo + 1))
                    sp.dma_start(raw[:, 0], w_qkv[g + 1, 0]).then_inc(raw_landed[0], 16)
                    sp.dma_start(raw[:, 1], w_qkv[g + 1, 1]).then_inc(raw_landed[1], 16)
                    sp.wait_ge(scores_ready, (g + 1) * (TB * HG))
                    sp.dma_start(decays[:, :, :], decay[:, bass.ds((g + 1) * HG, HG), :]).then_inc(decay_landed, 16)
                rest_of_group(GROUPS - 1)

            @block.gpsimd
            def _(pool):
                nc.gpsimd.memset(minus_half[:, :], -0.5).then_inc(consts_set, 1)
                nc.gpsimd.memset(ones[:, :], 1.0).then_inc(consts_set, 1)
                nc.gpsimd.memset(sq_acc[:, :], 0.0).then_inc(sq_made, HG)
                pool.wait_ge(consts_set, 2)
                for t in range(TILES):
                    pool.wait_ge(var_ready, t + 1)
                    nc.gpsimd.tensor_scalar(rstd[:, t % 2:t % 2 + 1], mv[:, t % 2, 1:2], EPS, None,
                                            ALU.add).then_inc(eps_added, 1)
                    pool.wait_ge(eps_added, t + 1)
                    nc.gpsimd.tensor_tensor(rstd[:, t % 2:t % 2 + 1], rstd[:, t % 2:t % 2 + 1], minus_half[:, :],
                                            ALU.pow).then_inc(rstd_ready, 1)
                pool.wait_ge(xn_ready, TILES)
                nc.gpsimd.memset(attn_acc[:, :, :], 0.0).then_inc(out_added, TT)

                def squares(g, tb, first=False):
                    for h in range(HG):
                        n = g * (TB * HG) + (tb * HG + h)
                        pool.wait_ge(attn_ready, n + 1)
                        pool.wait_ge(sq_made, n + HG)
                        if not (first and tb == 0 and h == 0):
                            pool.wait_ge(sq_added, n)
                        nc.gpsimd.tensor_tensor(sq[:, :], attn[:, h], attn[:, h], ALU.mult).then_inc(sq_made, 1)
                        pool.wait_ge(sq_made, n + HG + 1)
                        acc = sq_acc[:, tb * BT:(tb + 1) * BT]
                        nc.gpsimd.tensor_tensor(acc, acc, sq[:, :], ALU.add).then_inc(sq_added, 1)

                for tb in range(TB):
                    squares(0, tb, True)
                with nc.Fori(1, GROUPS, engines=[pool.engine], hint_back_edge=True) as g:
                    for tb in range(TB):
                        squares(g, tb)

            @block.scalar
            def _(act):
                def cut_hi(g, w):
                    ab, nth, per = ((0, (0, 0, 1, 0, 2)[w], 3) if w in (wq, wv, wo) else (1, (w - wk) // 2, 2))
                    act.wait_ge(raw_landed[ab], g * (16 * per) + 16 * (nth + 1))
                    if w == wo:
                        for h in range(HG):
                            i = nc.scalar.activation(w_hi[:, w, h * D:(h + 1) * D], raw[:, ab, h * D:(h + 1) * D],
                                                     ACT.Copy, scale=normw[:, bass.ds(g * HG + h, 1)])
                        i.then_inc(hi_cut, 1)
                    else:
                        nc.scalar.activation(w_hi[:, w], raw[:, ab], ACT.Copy).then_inc(hi_cut, 1)

                def sigmoids_qk(u):
                    for j in range(2 * HG):
                        act.wait_ge(qk_mm, u * (2 * HG) + (j + 1))
                        nc.scalar.activation(qk[:, j // HG, j % HG], bank[:, j], ACT.Sigmoid).then_inc(qk_sig, 1)

                def step(g, tb, last=False):
                    u = g * TB + tb
                    if tb == TB - 1 and not last:
                        act.wait_ge(v_mm, u * 2 + 1)
                        cut_hi(g + 1, wq)
                        cut_hi(g + 1, wk)
                    for j in range(2):
                        act.wait_ge(v_mm, u * 2 + (j + 1))
                        nc.scalar.activation(v[:, 2 * j:2 * j + 2], bank[:, j].rearrange("p (t n) -> p t n", t=2),
                                             ACT.Sigmoid).then_inc(v_sig, 1)
                    if tb == 0:
                        cut_hi(g, wo)
                    if tb == TB - 1 and not last:
                        cut_hi(g + 1, wv)
                    for h in range(HG):
                        act.wait_ge(g_mm, u * HG + (h + 1))
                        nc.scalar.activation(gate[:, h], bank[:, 4 + h], ACT.Sigmoid).then_inc(gate_ready, 1)
                    for h in range(HG):
                        act.wait_ge(pv_mm, u * HG + (h + 1))
                        act.wait_ge(sq_made, u * HG + (h + 1))
                        nc.scalar.activation(attn[:, h], bank[:, 6 + h], ACT.Copy).then_inc(attn_ready, 1)
                    if tb == TB - 1 and not last:
                        cut_hi(g + 1, wg)
                    for h in range(HG):
                        act.wait_ge(y_made, u * HG + (h + 1))
                        nc.scalar.activation(y_hi[:, h], gate[:, h], ACT.Copy).then_inc(y_hi_ready, 1)
                    if not (last and tb == TB - 1):
                        sigmoids_qk(u + 1)

                for t in range(TILES):
                    act.wait_ge(xn_turned, t + 1)
                    nc.scalar.activation(xn_hi[:, :, t * P:(t + 1) * P],
                                         bank[:, t % 4].rearrange("p (c n) -> p c n", c=CH),
                                         ACT.Copy).then_inc(xn_hi_ready, 1)
                    if t < 4:
                        cut_hi(0, t)
                act.wait_ge(normw_landed, 16)
                sigmoids_qk(0)
                with nc.Fori(0, GROUPS - 1, engines=[act.engine], hint_back_edge=True) as g:
                    for tb in range(TB):
                        step(g, tb)
                for tb in range(TB):
                    step(GROUPS - 1, tb, True)

            @block.vector
            def _(dve):
                def cut_lo(g, w):
                    ab = 0 if w in (wq, wv, wo) else 1
                    dve.wait_ge(hi_cut, g * 5 + (w + 1))
                    if w == wo:
                        for h in range(HG):
                            i = nc.vector.scalar_tensor_tensor(
                                out=w_lo[:, w, h * D:(h + 1) * D], in0=raw[:, ab, h * D:(h + 1) * D],
                                scalar=normw[:, bass.ds(g * HG + h, 1)],
                                in1=w_hi[:, w, h * D:(h + 1) * D].bitcast(F32), op0=ALU.mult, op1=ALU.subtract)
                    else:
                        i = nc.vector.tensor_tensor(w_lo[:, w], raw[:, ab], w_hi[:, w].bitcast(F32), ALU.subtract)
                    i.then_inc(w_ready, 1)

                def silus_qk(u):
                    for j in range(2 * HG):
                        dve.wait_ge(qk_sig, u * (2 * HG) + (j + 1))
                        o = qk[:, j // HG, j % HG]
                        nc.vector.tensor_tensor(o, bank[:, j], o, ALU.mult).then_inc(qk_ready, 1)

                def step(g, tb, last=False):
                    u = g * TB + tb
                    if tb == TB - 1 and not last:
                        cut_lo(g + 1, wq)
                        cut_lo(g + 1, wk)
                    for j in range(2):
                        dve.wait_ge(v_sig, u * 2 + (j + 1))
                        o = v[:, 2 * j:2 * j + 2]
                        nc.vector.tensor_tensor(o, bank[:, j].rearrange("p (t n) -> p t n", t=2), o,
                                                ALU.mult).then_inc(v_ready, 1)
                    if tb == 0:
                        cut_lo(g, wo)
                        dve.wait_ge(decay_landed, g * 16 + 16)
                    for h in range(HG):
                        dve.wait_ge(s_mm, u * HG + (h + 1))
                        nc.vector.tensor_tensor(scores[:, h].rearrange("p (t n) -> p t n", t=TT),
                                                bank[:, 2 + h].rearrange("p (t n) -> p t n", t=TT),
                                                decays[:, h:h + 1].broadcast_to([P, TT, P]),
                                                ALU.mult).then_inc(scores_ready, 1)
                    if tb == TB - 1 and not last:
                        cut_lo(g + 1, wv)
                    for h in range(HG):
                        dve.wait_ge(attn_ready, u * HG + (h + 1))
                        nc.vector.tensor_tensor(gate[:, h], gate[:, h], attn[:, h], ALU.mult).then_inc(y_made, 1)
                    for h in range(HG):
                        dve.wait_ge(y_hi_ready, u * HG + (h + 1))
                        nc.vector.tensor_tensor(y_lo[:, h], gate[:, h], y_hi[:, h].bitcast(F32),
                                                ALU.subtract).then_inc(y_ready, 1)
                    if tb == TB - 1 and not last:
                        cut_lo(g + 1, wg)
                    if not (last and tb == TB - 1):
                        silus_qk(u + 1)
                    for i in range(TT):
                        dve.wait_ge(out_mm, u * TT + (i + 1))
                        acc = attn_acc[:, tb * TT + i]
                        nc.vector.tensor_tensor(acc, acc, bank[:, 4 + i], ALU.add).then_inc(out_added, 1)

                def lo(t):
                    dve.wait_ge(xn_hi_ready, t + 1)
                    s = slice(t * P, (t + 1) * P)
                    nc.vector.tensor_tensor(xn_lo[:, :, s], bank[:, t % 4].rearrange("p (c n) -> p c n", c=CH),
                                            xn_hi[:, :, s].bitcast(F32), ALU.subtract).then_inc(xn_lo_ready, 1)

                def statistics(t):
                    if t % TT == 0:
                        dve.wait_ge(x_landed[t // TT], 16)
                    nc.vector.bn_stats(stats[:, t % 2], attn_acc[:, t]).then_inc(stats_done, 1)
                    dve.wait_ge(stats_done, t + 1)
                    nc.vector.bn_aggr(mv[:, t % 2], stats[:, t % 2]).then_inc(var_ready, 1)

                statistics(0)
                for t in range(TILES):
                    if t + 1 < TILES:
                        statistics(t + 1)
                    dve.wait_ge(rstd_ready, t + 1)
                    if t >= 2:
                        dve.wait_ge(xn_turned, t - 1)
                    nc.vector.tensor_scalar(xn[:, t % 2], attn_acc[:, t], mv[:, t % 2, 0:1],
                                            rstd[:, t % 2:t % 2 + 1], ALU.subtract, ALU.mult).then_inc(xn_ready, 1)
                    if t >= 1:
                        lo(t - 1)
                    if 1 <= t < 5:
                        cut_lo(0, t - 1)
                lo(TILES - 1)
                silus_qk(0)
                with nc.Fori(0, GROUPS - 1, engines=[dve.engine], hint_back_edge=True) as g:
                    for tb in range(TB):
                        step(g, tb)
                for tb in range(TB):
                    step(GROUPS - 1, tb, True)

            @block.tensor
            def _(pe):
                def weights(half, w, c, h):
                    return half[:, w, c * HG * HD + h * HD:c * HG * HD + (h + 1) * HD]

                def project(dst, w, h, tb, done):
                    s = slice(tb * BT, (tb + 1) * BT)
                    for c in range(CH):
                        hi = weights(w_hi, w, c, h)
                        nc.tensor.matmul(dst, hi, xn_hi[:, c, s], start=(c == 0), stop=False)
                        nc.tensor.matmul(dst, hi, xn_lo[:, c, s], start=False, stop=False)
                        i = nc.tensor.matmul(dst, weights(w_lo, w, c, h), xn_hi[:, c, s],
                                             start=False, stop=(c == CH - 1))
                    i.then_inc(done, 1)

                def project_qk(g, tb):
                    for j in range(2 * HG):
                        if tb == 0 and j % HG == 0:
                            pe.wait_ge(w_ready, g * 5 + (j // HG + 1))
                        project(bank[:, j], j // HG, j % HG, tb, qk_mm)

                def step(g, tb, last=False):
                    u = g * TB + tb
                    pe.wait_ge(qk_ready, u * (2 * HG) + 2)
                    if tb == 0:
                        pe.wait_ge(w_ready, g * 5 + wv + 1)
                    for i in range(TT):
                        dst = bank[:, i // 2, (i % 2) * HG * HD:(i % 2 + 1) * HG * HD]
                        s = slice(tb * BT + i * P, tb * BT + (i + 1) * P)
                        for c in range(CH):
                            m = slice(c * HG * HD, (c + 1) * HG * HD)
                            nc.tensor.matmul(dst, xn_hi[:, c, s], w_hi[:, wv, m], start=(c == 0), stop=False)
                            nc.tensor.matmul(dst, xn_hi[:, c, s], w_lo[:, wv, m], start=False, stop=False)
                            k = nc.tensor.matmul(dst, xn_lo[:, c, s], w_hi[:, wv, m], start=False, stop=(c == CH - 1))
                        if i % 2:
                            k.then_inc(v_mm, 1)
                    pe.wait_ge(qk_ready, u * (2 * HG) + 2 * HG)
                    for h in range(HG):
                        for i in range(TT):
                            s = slice(i * P, (i + 1) * P)
                            k = nc.tensor.matmul(bank[:, 2 + h, s], qk[:, 1, h, s], qk[:, 0, h, s],
                                                 start=True, stop=True)
                        k.then_inc(s_mm, 1)
                    if tb == 0:
                        pe.wait_ge(w_ready, g * 5 + wg + 1)
                    for h in range(HG):
                        if h == 0:
                            pe.wait_ge(out_added, u * TT + 2)
                        project(bank[:, 4 + h], wg, h, tb, g_mm)
                    pe.wait_ge(v_ready, u * 2 + 2)
                    pe.wait_ge(out_added, u * TT + TT)
                    for h in range(HG):
                        pe.wait_ge(scores_ready, u * HG + (h + 1))
                        for i in range(TT):
                            s = slice(i * P, (i + 1) * P)
                            k = nc.tensor.matmul(bank[:, 6 + h, s], v[:, i, h * HD:(h + 1) * HD], scores[:, h, s],
                                                 start=True, stop=True)
                        k.then_inc(pv_mm, 1)
                    if not (last and tb == TB - 1):
                        project_qk(g if tb < TB - 1 else g + 1, (tb + 1) % TB)
                    if tb == 0:
                        pe.wait_ge(w_ready, g * 5 + wo + 1)
                    pe.wait_ge(y_ready, u * HG + HG)
                    for i in range(TT):
                        s = slice(i * P, (i + 1) * P)
                        for h in range(HG):
                            m = slice(h * D, (h + 1) * D)
                            nc.tensor.matmul(bank[:, 4 + i], y_hi[:, h, s], w_hi[:, wo, m], start=(h == 0), stop=False)
                            nc.tensor.matmul(bank[:, 4 + i], y_hi[:, h, s], w_lo[:, wo, m], start=False, stop=False)
                            k = nc.tensor.matmul(bank[:, 4 + i], y_lo[:, h, s], w_hi[:, wo, m],
                                                 start=False, stop=(h == HG - 1))
                        k.then_inc(out_mm, 1)

                pe.wait_ge(const_landed, 16)
                for t in range(TILES):
                    pe.wait_ge(xn_ready, t + 1)
                    if t >= 4:
                        pe.wait_ge(xn_lo_ready, t - 3)
                    for c in range(CH):
                        s = slice(c * P, (c + 1) * P)
                        k = nc.tensor.transpose(bank[:, t % 4, s], xn[:, t % 2, s], ident[:, :])
                    k.then_inc(xn_turned, 1)
                pe.wait_ge(xn_lo_ready, TILES)
                project_qk(0, 0)
                with nc.Fori(0, GROUPS - 1, engines=[pe.engine], hint_back_edge=True) as g:
                    for tb in range(TB):
                        step(g, tb)
                for tb in range(TB):
                    step(GROUPS - 1, tb, True)


def cross_and_ffn(nc, sb, sem, bank, x1, sq_acc, ident, ones, x, ctx_in, wq_in, wk_in, wv_in, bq_in, bk_in, bv_in,
                  eye_in, out):
    with ExitStack() as own:
        xr = sb(own, "xr", [P, TILES, D])
        ms = sb(own, "ms", [P, TILES])
        rrms = sb(own, "rrms", [P, TILES])
        minus_half = sb(own, "minus_half2", [P, TILES])
        ctx = sb(own, "ctx", [P, 2, D])
        ctx_parts = sb(own, "ctx_parts", [P, 2, D], F32R)
        wqk = sb(own, "wqk", [P, 2, P])
        wqk_hi = sb(own, "wqk_hi", [P, 2, P], F32R)
        wqk_lo = sb(own, "wqk_lo", [P, 2, P], F32R)
        bqk = sb(own, "bqk", [P, 2])
        wv = sb(own, "wv", [P, P])
        bv = sb(own, "bv", [P, P])
        q_parts = sb(own, "q_parts", [P, 2, D], F32R)
        k_hi = sb(own, "k_hi", [P, 2, D], F32R)
        k_lo = sb(own, "k_lo", [P, 2, D], F32R)
        minus_max = sb(own, "minus_max", [P, 2, CH])
        row_sum = sb(own, "row_sum", [P, 2, CH])
        row_inv = sb(own, "row_inv", [P, 2, CH])
        prob = sb(own, "prob", [P, 2, CH, D])
        probT_hi = sb(own, "probT_hi", [P, 2, D], F32R)
        probT_lo = sb(own, "probT_lo", [P, 2, D], F32R)
        xn2 = sb(own, "xn2", [P, D])
        v32 = sb(own, "v32", [P, CH, 2, SEQ])
        v_hi = sb(own, "v_hi", [P, CH, 2, P], F32R)
        v_lo = sb(own, "v_lo", [P, CH, 2, P], F32R)
        xn3 = sb(own, "xn3", [P, D])
        xn3_hi = sb(own, "xn3_hi", [P, CH, P], F32R)
        xn3_lo = sb(own, "xn3_lo", [P, CH, P], F32R)
        eye = sb(own, "eye", [P, CH, D])
        eye_hi = sb(own, "eye_hi", [P, CH, D], F32R)
        eye_lo = sb(own, "eye_lo", [P, CH, D], F32R)
        stats = sb(own, "stats2", [P, 2, 6])
        mv = sb(own, "mv2", [P, 2, 2])
        rstd = sb(own, "rstd2", [P, 2])
        shift = sb(own, "shift", [P, 2])

        names = """summed ms_ready rrms_ready x1_ready consts_landed eye_landed consts_set wqk_hi_cut wqk_cut
            eye_hi_cut eye_cut ctx_hi_ready ctx_ready qk_mm qk_hi_ready qk_ready r_mm max_ready exp_ready inv_ready
            prob_pool prob_dve turned probT_hi_ready probT_ready pv_mm x2_ready ln2_stats ln2_var ln2_eps ln2_root ln2_rstd xn2_ready
            v_mm v_made v_hi_ready v_ready ln3_stats ln3_var ln3_eps ln3_root ln3_rstd xn3_ready xn3_turned xn3_hi_ready
            xn3T_ready ffn_mm out_ready stored""".split()
        S = {n: sem("b_" + n) for n in names}
        passed = sem("passed")
        x_back = [sem(f"x_back{i}") for i in range(TB)]
        ctx_landed = [sem(f"ctx_landed{i}") for i in range(2)]
        x_t = x.rearrange("b s d -> (b s) d").rearrange("(k t p) d -> k p t d", t=TT, p=P)
        out_t = out.rearrange("b s d -> (b s) d").rearrange("(t p) d -> t p d", p=P)
        PAIRS = TILES
        Q, K, OUT, MISC = 4, 5, 6, 7

        with nc.Block() as block:

            @block.sync
            def _(sp):
                def load_ctx(b, i):
                    for half in range(2):
                        sp.dma_start(ctx[half * SEQ:(half + 1) * SEQ, i], ctx_in[b]).then_inc(ctx_landed[i], 16)

                for i in range(2):
                    load_ctx(i, i)
                for dst, src in ((wqk[:, 0], wq_in), (wqk[:, 1], wk_in), (bqk[:, 0:1], bq_in), (bqk[:, 1:2], bk_in),
                                 (wv[:, :], wv_in), (bv[:, :], bv_in)):
                    sp.dma_start(dst, src).then_inc(S["consts_landed"], 16)
                for k in range(TB):
                    sp.dma_start(xr[:, k * TT:(k + 1) * TT], x_t[k]).then_inc(x_back[k], 16)
                sp.dma_start(eye[:, :, :], eye_in).then_inc(S["eye_landed"], 16)

                def store(t):
                    sp.wait_ge(S["out_ready"], t + 1)
                    sp.dma_start(out_t[t], x1[:, t]).then_inc(S["stored"], 16)

                def pair(t, first=False):
                    for i in range(2):
                        sp.wait_ge(S["ctx_ready"], t * 2 + (i + 1))
                        load_ctx(t * 2 + (2 + i), i)
                    if not first:
                        store(t - 2)

                pair(0, True)
                pair(1, True)
                with nc.Fori(2, PAIRS - 1, engines=[sp.engine], hint_back_edge=True) as t:
                    pair(t)
                store(PAIRS - 3)
                store(PAIRS - 2)
                store(PAIRS - 1)
                sp.wait_ge(S["stored"], 16 * PAIRS)

            @block.gpsimd
            def _(pool):
                nc.gpsimd.memset(minus_half[:, :], -0.5).then_inc(S["consts_set"], 1)
                nc.gpsimd.memset(v_hi[:, :, :, :].bitcast(F32), 0.0).then_inc(S["consts_set"], 1)
                nc.gpsimd.memset(v_lo[:, :, :, :].bitcast(F32), 0.0).then_inc(S["consts_set"], 1)
                pool.wait_ge(S["consts_set"], 3)

                def ctx_lo(b, i):
                    pool.wait_ge(S["ctx_hi_ready"], b + 1)
                    lo = slice(SEQ, P)
                    nc.gpsimd.tensor_tensor(ctx_parts[lo, i], ctx[lo, i], ctx_parts[lo, i].bitcast(F32),
                                            ALU.subtract).then_inc(S["ctx_ready"], 1)
                    pool.wait_ge(S["ctx_ready"], b + 1)

                def inv_root(n, k, t):
                    wait_apart(pool, S[f"ln{n}_var"], t + 1, passed)
                    nc.gpsimd.tensor_scalar(rstd[:, k:k + 1], mv[:, k, 1:2], EPS, None,
                                            ALU.add).then_inc(S[f"ln{n}_eps"], 1)
                    pool.wait_ge(S[f"ln{n}_eps"], t + 1)
                    nc.gpsimd.tensor_tensor(rstd[:, k:k + 1], rstd[:, k:k + 1], minus_half[:, 0:1],
                                            ALU.pow).then_inc(S[f"ln{n}_root"], 1)
                    wait_apart(pool, S[f"ln{n}_root"], t + 1, passed)
                    nc.gpsimd.tensor_scalar(shift[:, k:k + 1], mv[:, k, 0:1], rstd[:, k:k + 1], -1.0, ALU.mult,
                                            ALU.mult).then_inc(S[f"ln{n}_rstd"], 1)

                def normalise(b, i, tiles=range(3)):
                    for j in tiles:
                        wait_apart(pool, S["inv_ready"], b * CH + (j + 1), passed)
                        nc.gpsimd.tensor_scalar(prob[:, i, j], prob[:, i, j], row_inv[:, i, j:j + 1], None,
                                                ALU.mult).then_inc(S["prob_pool"], 1)

                def pair(t, first=False, last=False, more_pairs=True):
                    for i in range(2):
                        b = t * 2 + i
                        if not (last and i == 1):
                            normalise(b + 1, 1 - i, range(2))
                        if i == 0 and not first:
                            inv_root(3, 1, t - 1)
                        if not (last and i == 1):
                            normalise(b + 1, 1 - i, range(2, 3))
                        if i == 0 and not last or i == 1 and more_pairs:
                            pool.wait_ge(S["prob_pool"], b * 3 + 6)
                            ctx_lo(b + 3, 1 - i)
                        if i == 1 and more_pairs:
                            inv_root(2, 0, t + 2)

                ctx_lo(0, 0)
                ctx_lo(1, 1)
                pool.wait_ge(S["ms_ready"], 1)
                nc.gpsimd.tensor_tensor(rrms[:, :], ms[:, :], minus_half[:, :], ALU.pow).then_inc(S["rrms_ready"], 1)
                inv_root(2, 0, 0)
                normalise(0, 0)
                pool.wait_ge(S["prob_pool"], 3)
                ctx_lo(2, 0)
                inv_root(2, 0, 1)
                pair(0, first=True)
                with nc.Fori(1, PAIRS - 2, engines=[pool.engine], hint_back_edge=True) as t:
                    pair(t)
                pair(PAIRS - 2, more_pairs=False)
                pair(PAIRS - 1, last=True, more_pairs=False)
                inv_root(3, 1, PAIRS - 1)

            @block.scalar
            def _(act):
                def ctx_hi(b, i, nth):
                    act.wait_ge(ctx_landed[i], nth * 32)
                    nc.scalar.activation(ctx_parts[:, i], ctx[:, i], ACT.Copy).then_inc(S["ctx_hi_ready"], 1)

                def qk_hi(b, i, which=range(2)):
                    for j in which:
                        dst = (q_parts, k_hi)[j]
                        act.wait_ge(S["qk_mm"], b * 2 + (j + 1))
                        nc.scalar.activation(dst[:, i], bank[:, Q + j], ACT.Identity,
                                             bias=bqk[:, j:j + 1]).then_inc(S["qk_hi_ready"], 1)

                def normed(n, k, t, dst):
                    act.wait_ge(S[f"ln{n}_rstd"], t + 1)
                    nc.scalar.activation(dst[:, :], x1[:, t], ACT.Identity, bias=shift[:, k:k + 1],
                                         scale=rstd[:, k:k + 1]).then_inc(S[f"xn{n}_ready"], 1)

                def exps(b, i, j):
                    act.wait_ge(S["max_ready"], b * CH + (j + 1))
                    nc.scalar.activation(prob[:, i, j], bank[:, j % 2], ACT.Exp, bias=minus_max[:, i, j:j + 1],
                                         accum_out=row_sum[:, i, j:j + 1]).then_inc(S["exp_ready"], 1)

                def turned_hi(b, j):
                    act.wait_ge(S["turned"], b * CH + (j + 1))
                    nc.scalar.activation(probT_hi[:, j % 2], bank[:, 2 + j % 2], ACT.Copy)\
                        .then_inc(S["probT_hi_ready"], 1)

                def v_high(t, i, first=False):
                    if i == 0:
                        act.wait_ge(S["v_made"], t + 1)
                    elif not first:
                        act.wait_ge(S["pv_mm"], t)
                    nc.scalar.activation(v_hi[:, :, i, 0:SEQ], v32[:, :, i], ACT.Copy).then_inc(S["v_hi_ready"], 1)

                def xn3_high(t):
                    act.wait_ge(S["xn3_turned"], t + 1)
                    nc.scalar.activation(xn3_hi[:, :, :], bank[:, MISC].rearrange("p (c n) -> p c n", c=CH),
                                         ACT.Copy).then_inc(S["xn3_hi_ready"], 1)

                def pair(t, first=False, last=False, more_pairs=True):
                    for i in range(2):
                        b = t * 2 + i
                        more = not (last and i == 1)
                        turned_hi(b, 0)
                        if i == 0:
                            v_high(t, 0)
                        if i == 1 and not first:
                            xn3_high(t - 1)
                        if more:
                            exps(b + 1, 1 - i, 1)
                        if i == 0 and not last or i == 1 and more_pairs:
                            ctx_hi(b + 3, 1 - i, t + (2 + i))
                        turned_hi(b, 1)
                        if not last:
                            qk_hi(b + 2, i, range(1))
                        if more:
                            exps(b + 1, 1 - i, 2)
                        if not last:
                            qk_hi(b + 2, i, range(1, 2))
                        turned_hi(b, 2)
                        if i == 0:
                            v_high(t, 1, first)
                        if more:
                            exps(b + 1, 1 - i, 3)
                        if i == 0 and not first:
                            normed(3, 1, t - 1, xn3)
                        turned_hi(b, 3)
                        if i == 0 and not last:
                            normed(2, 0, t + 1, xn2)
                        if not last:
                            exps(b + 2, i, 0)

                act.wait_ge(S["consts_landed"], 16 * 6)
                nc.scalar.activation(wqk_hi[:, :, :], wqk[:, :, :], ACT.Copy).then_inc(S["wqk_hi_cut"], 1)
                ctx_hi(0, 0, 1)
                ctx_hi(1, 1, 1)
                qk_hi(0, 0)
                for j in range(CH):
                    exps(0, 0, j)
                qk_hi(1, 1)
                exps(1, 1, 0)
                ctx_hi(2, 0, 2)
                act.wait_ge(S["consts_set"], 3)
                act.wait_ge(S["eye_landed"], 16)
                nc.scalar.activation(eye_hi[:, :, :], eye[:, :, :], ACT.Copy).then_inc(S["eye_hi_cut"], 1)
                normed(2, 0, 0, xn2)
                pair(0, first=True)
                with nc.Fori(1, PAIRS - 2, engines=[act.engine], hint_back_edge=True) as t:
                    pair(t)
                pair(PAIRS - 2, more_pairs=False)
                pair(PAIRS - 1, last=True, more_pairs=False)
                normed(3, 1, PAIRS - 1, xn3)
                xn3_high(PAIRS - 1)

            @block.vector
            def _(dve):
                def qk_lo(b, i):
                    lo = slice(SEQ, P)
                    dve.wait_ge(S["qk_hi_ready"], b * 2 + 1)
                    nc.vector.scalar_tensor_tensor(out=q_parts[lo, i], in0=bank[lo, Q], scalar=bqk[lo, 0:1],
                                                   in1=q_parts[lo, i].bitcast(F32), op0=ALU.add,
                                                   op1=ALU.subtract).then_inc(S["qk_ready"], 1)
                    dve.wait_ge(S["qk_hi_ready"], b * 2 + 2)
                    nc.vector.scalar_tensor_tensor(out=k_lo[:, i], in0=bank[:, K], scalar=bqk[:, 1:2],
                                                   in1=k_hi[:, i].bitcast(F32), op0=ALU.add,
                                                   op1=ALU.subtract).then_inc(S["qk_ready"], 1)

                def row_max(b, i, j):
                    dve.wait_ge(S["r_mm"], b * CH + (j + 1))
                    nc.vector.tensor_reduce(minus_max[:, i, j:j + 1], bank[:, j % 2], AX.X, ALU.max,
                                            negate=True).then_inc(S["max_ready"], 1)

                def inverse(b, i, j):
                    dve.wait_ge(S["exp_ready"], b * CH + (j + 1))
                    nc.vector.reciprocal(row_inv[:, i, j:j + 1], row_sum[:, i, j:j + 1]).then_inc(S["inv_ready"], 1)

                def normalise(b, i):
                    dve.wait_ge(S["inv_ready"], b * CH + CH)
                    nc.vector.tensor_scalar(prob[:, i, 3], prob[:, i, 3], row_inv[:, i, 3:4], None,
                                            ALU.mult).then_inc(S["prob_dve"], 1)

                def turned_lo(b, j):
                    dve.wait_ge(S["probT_hi_ready"], b * CH + (j + 1))
                    nc.vector.tensor_tensor(probT_lo[:, j % 2], bank[:, 2 + j % 2], probT_hi[:, j % 2].bitcast(F32),
                                            ALU.subtract).then_inc(S["probT_ready"], 1)

                def make_x1(t):
                    nc.vector.scalar_tensor_tensor(out=x1[:, t], in0=x1[:, t], scalar=rrms[:, bass.ds(t, 1)],
                                                   in1=xr[:, t], op0=ALU.mult, op1=ALU.add)\
                        .then_inc(S["x1_ready"], 1)
                    wait_apart(dve, S["x1_ready"], t + 1, passed)

                def layernorm(n, k, t):
                    nc.vector.bn_stats(stats[:, k], x1[:, t]).then_inc(S[f"ln{n}_stats"], 1)
                    wait_apart(dve, S[f"ln{n}_stats"], t + 1, passed)
                    nc.vector.bn_aggr(mv[:, k], stats[:, k]).then_inc(S[f"ln{n}_var"], 1)

                def make_v(t):
                    dve.wait_ge(S["v_mm"], t + 1)
                    nc.vector.tensor_tensor(v32[:, :, :, :].rearrange("p c b o -> p c (b o)"),
                                            bank[:, MISC].rearrange("p (c n) -> p c n", c=CH),
                                            bv[:, :].rearrange("p (a n) -> p a n", a=1).broadcast_to([P, CH, P]),
                                            ALU.add).then_inc(S["v_made"], 1)

                def xn3_low(t):
                    dve.wait_ge(S["xn3_hi_ready"], t + 1)
                    nc.vector.tensor_tensor(xn3_lo[:, :, :], bank[:, MISC].rearrange("p (c n) -> p c n", c=CH),
                                            xn3_hi[:, :, :].bitcast(F32), ALU.subtract).then_inc(S["xn3T_ready"], 1)

                def add_cross(t):
                    dve.wait_ge(S["pv_mm"], t + 1)
                    nc.vector.tensor_tensor(x1[:, t], x1[:, t], bank[:, OUT], ALU.add).then_inc(S["x2_ready"], 1)
                    wait_apart(dve, S["x2_ready"], t + 1, passed)

                def add_ffn(t):
                    dve.wait_ge(S["ffn_mm"], t + 1)
                    nc.vector.tensor_tensor(x1[:, t], x1[:, t], bank[:, MISC], ALU.add).then_inc(S["out_ready"], 1)

                def v_low(t, i):
                    dve.wait_ge(S["v_hi_ready"], t * 2 + (i + 1))
                    nc.vector.tensor_tensor(v_lo[:, :, i, 0:SEQ], v32[:, :, i], v_hi[:, :, i, 0:SEQ].bitcast(F32),
                                            ALU.subtract).then_inc(S["v_ready"], 1)

                def pair(t, first=False, last=False, more_pairs=True):
                    for i in range(2):
                        b = t * 2 + i
                        more = not (last and i == 1)
                        if more:
                            inverse(b + 1, 1 - i, 0)
                            row_max(b + 1, 1 - i, 1)
                        turned_lo(b, 0)
                        if i == 0:
                            v_low(t, 0)
                        if i == 0 and not first:
                            add_cross(t - 1)
                            layernorm(3, 1, t - 1)
                        if i == 1 and not first:
                            xn3_low(t - 1)
                        if i == 1 and more_pairs:
                            wait_apart(dve, S["xn2_ready"], t + 2, passed)
                            layernorm(2, 0, t + 2)
                        if more:
                            inverse(b + 1, 1 - i, 1)
                            row_max(b + 1, 1 - i, 2)
                        turned_lo(b, 1)
                        if not last:
                            qk_lo(b + 2, i)
                        if more:
                            inverse(b + 1, 1 - i, 2)
                            row_max(b + 1, 1 - i, 3)
                        turned_lo(b, 2)
                        if i == 0:
                            v_low(t, 1)
                        if i == 1 and not first:
                            add_ffn(t - 1)
                        if more:
                            inverse(b + 1, 1 - i, 3)
                            normalise(b + 1, 1 - i)
                        if not last:
                            row_max(b + 2, i, 0)
                        turned_lo(b, 3)
                        if i == 0 and more_pairs:
                            make_x1(t + 2)
                    if not last:
                        make_v(t + 1)

                dve.wait_ge(S["wqk_hi_cut"], 1)
                nc.vector.tensor_tensor(wqk_lo[:, :, :], wqk[:, :, :], wqk_hi[:, :, :].bitcast(F32),
                                        ALU.subtract).then_inc(S["wqk_cut"], 1)
                dve.wait_ge(S["summed"], 1)
                nc.vector.tensor_scalar(ms[:, :], bank[:, MISC, 0:TILES], 1.0 / (HEADS * HD), EPS, ALU.mult,
                                        ALU.add).then_inc(S["ms_ready"], 1)
                qk_lo(0, 0)
                for j in range(CH):
                    row_max(0, 0, j)
                    inverse(0, 0, j)
                normalise(0, 0)
                qk_lo(1, 1)
                row_max(1, 1, 0)
                dve.wait_ge(S["rrms_ready"], 1)
                for k in range(TB):
                    dve.wait_ge(x_back[k], 16)
                make_x1(0)
                layernorm(2, 0, 0)
                make_x1(1)
                dve.wait_ge(S["xn2_ready"], 1)
                layernorm(2, 0, 1)
                make_v(0)
                dve.wait_ge(S["eye_hi_cut"], 1)
                nc.vector.tensor_tensor(eye_lo[:, :, :], eye[:, :, :], eye_hi[:, :, :].bitcast(F32),
                                        ALU.subtract).then_inc(S["eye_cut"], 1)
                pair(0, first=True)
                with nc.Fori(1, PAIRS - 2, engines=[dve.engine], hint_back_edge=True) as t:
                    pair(t)
                pair(PAIRS - 2, more_pairs=False)
                pair(PAIRS - 1, last=True, more_pairs=False)
                add_cross(PAIRS - 1)
                layernorm(3, 1, PAIRS - 1)
                xn3_low(PAIRS - 1)
                add_ffn(PAIRS - 1)

            @block.tensor
            def _(pe):
                def project(b, i):
                    pe.wait_ge(S["ctx_ready"], b + 1)
                    for j in range(2):
                        nc.tensor.matmul(bank[:, Q + j], wqk_hi[:, j], ctx_parts[:, i], start=True, stop=False)
                        nc.tensor.matmul(bank[:, Q + j], wqk_lo[:, j], ctx_parts[:, i], start=False,
                                         stop=True).then_inc(S["qk_mm"], 1)

                def cross_scores(b, i, j, begun=True):
                    if begun:
                        pe.wait_ge(S["exp_ready"], b * CH + (j - 1))
                    if j == 0:
                        pe.wait_ge(S["qk_ready"], b * 2 + 2)
                    q = q_parts[:, i, j * P:(j + 1) * P]
                    nc.tensor.matmul(bank[:, j % 2], q, k_hi[:, i], start=True, stop=False)
                    nc.tensor.matmul(bank[:, j % 2], q, k_lo[:, i], start=False, stop=True).then_inc(S["r_mm"], 1)

                def turn(b, i, j):
                    if j == 0:
                        pe.wait_ge(S["prob_pool"], b * 3 + 3)
                        pe.wait_ge(S["prob_dve"], b + 1)
                    for k in range(CH):
                        m = nc.tensor.transpose(bank[:, 2 + j % 2, k * P:(k + 1) * P],
                                                prob[:, i, k, j * P:(j + 1) * P], ident[:, :])
                    m.then_inc(S["turned"], 1)

                def weigh(b, i, j):
                    pe.wait_ge(S["probT_ready"], b * CH + (j + 1))
                    cols = slice(i * SEQ, i * SEQ + P)
                    vh = v_hi[:, j].rearrange("p b o -> p (b o)")[:, cols]
                    vl = v_lo[:, j].rearrange("p b o -> p (b o)")[:, cols]
                    nc.tensor.matmul(bank[:, OUT], vh, probT_hi[:, j % 2], start=(i == 0 and j == 0), stop=False)
                    nc.tensor.matmul(bank[:, OUT], vh, probT_lo[:, j % 2], start=False, stop=False)
                    m = nc.tensor.matmul(bank[:, OUT], vl, probT_hi[:, j % 2], start=False,
                                         stop=(i == 1 and j == CH - 1))
                    if i == 1 and j == CH - 1:
                        m.then_inc(S["pv_mm"], 1)

                def values(t, first=False):
                    pe.wait_ge(S["xn2_ready"], t + 1)
                    if not first:
                        pe.wait_ge(S["out_ready"], t - 1)
                    for c in range(CH):
                        m = nc.tensor.matmul(bank[:, MISC, c * P:(c + 1) * P], xn2[:, c * P:(c + 1) * P], wv[:, :],
                                             start=True, stop=True)
                    m.then_inc(S["v_mm"], 1)

                def turn_xn3(t):
                    pe.wait_ge(S["xn3_ready"], t + 1)
                    for c in range(CH):
                        s = slice(c * P, (c + 1) * P)
                        m = nc.tensor.transpose(bank[:, MISC, s], xn3[:, s], ident[:, :])
                    m.then_inc(S["xn3_turned"], 1)

                def ffn(t, chunks=range(CH)):
                    if 0 in chunks:
                        pe.wait_ge(S["xn3T_ready"], t + 1)
                    for c in chunks:
                        nc.tensor.matmul(bank[:, MISC], xn3_hi[:, c], eye_hi[:, c], start=(c == 0), stop=False)
                        nc.tensor.matmul(bank[:, MISC], xn3_hi[:, c], eye_lo[:, c], start=False, stop=False)
                        m = nc.tensor.matmul(bank[:, MISC], xn3_lo[:, c], eye_hi[:, c], start=False,
                                             stop=(c == CH - 1))
                    if CH - 1 in chunks:
                        m.then_inc(S["ffn_mm"], 1)

                def pair(t, first=False, last=False):
                    for i in range(2):
                        b = t * 2 + i
                        more = not (last and i == 1)
                        for j in range(CH):
                            turn(b, i, j)
                            if j == 0 and not (first and i == 0):
                                weigh(b - 1, 1 - i, CH - 1)
                            if j < CH - 1 and more:
                                cross_scores(b + 1, 1 - i, j + 1)
                            if j == CH - 1 and not last:
                                cross_scores(b + 2, i, 0)
                            if j == 0 and not last:
                                project(b + 2, i)
                            if j == 1:
                                pe.wait_ge(S["v_ready"], t * 2 + (i + 1))
                                if i == 0 and not first:
                                    pe.wait_ge(S["x2_ready"], t)
                            if j:
                                weigh(b, i, j - 1)
                            if (i, j) == (0, 3) and not first:
                                turn_xn3(t - 1)
                            if i == 1 and j in (1, 2) and not first:
                                ffn(t - 1, range(CH // 2 * (j - 1), CH // 2 * j))
                            if (i, j) == (1, 3) and not last:
                                values(t + 1, first)

                for t in range(TILES):
                    m = nc.tensor.matmul(bank[:, MISC, t:t + 1], sq_acc[:, t * P:(t + 1) * P], ones[:, 0:1],
                                         start=True, stop=True)
                m.then_inc(S["summed"], 1)
                pe.wait_ge(S["wqk_cut"], 1)
                project(0, 0)
                for j in range(CH):
                    cross_scores(0, 0, j, j >= 2)
                project(1, 1)
                cross_scores(1, 1, 0)
                pe.wait_ge(S["ms_ready"], 1)
                values(0, True)
                pe.wait_ge(S["eye_cut"], 1)
                pair(0, first=True)
                with nc.Fori(1, PAIRS - 1, engines=[pe.engine], hint_back_edge=True) as t:
                    pair(t)
                pair(PAIRS - 1, last=True)
                weigh(2 * PAIRS - 1, 1, CH - 1)
                turn_xn3(PAIRS - 1)
                ffn(PAIRS - 1)


def kernel(x, ctx_4096, L0_attn_qkv_w, L0_attn_out_w, L0_attn_gate_w, L0_attn_norm_w, L0_xattn_Wq, L0_xattn_bq,
           L0_xattn_Wk, L0_xattn_bk, L0_xattn_Wv, L0_xattn_bv, L0_ffn_identity):
    import concourse.bacc as bacc
    from concourse.bass_utils import run_bass_kernel_spmd

    def rows(w):
        w = w.reshape(GROUPS, HG, HD, CH, P).transpose(0, 4, 3, 1, 2)
        return np.ascontiguousarray(w.reshape(GROUPS, P, CH * HG * HD))

    qkv = np.asarray(L0_attn_qkv_w).reshape(HEADS, 3, HD, D)
    arrays = {
        "x": np.asarray(x),
        "ctx_in": np.asarray(ctx_4096),
        "w_qkv": np.ascontiguousarray(np.stack([rows(qkv[:, i]) for i in range(3)], axis=1)),
        "w_gate": rows(np.asarray(L0_attn_gate_w)),
        "w_out": np.ascontiguousarray(np.asarray(L0_attn_out_w).reshape(D, GROUPS, HG, HD).transpose(1, 3, 2, 0)
                                      .reshape(GROUPS, HD, HG * D)),
        "norm_w": np.ascontiguousarray(np.asarray(L0_attn_norm_w).reshape(HEADS, HD).T),
        "decay": decay_table(),
        "ident_in": np.eye(P, dtype=np.float32),
    }
    twice = lambda w: np.tile(np.asarray(w).T, (2, 2))
    column = lambda v: np.ascontiguousarray(np.tile(np.asarray(v), 2)[:, None])
    wv = np.zeros((P, P), np.float32)
    wv[:SEQ, :SEQ] = wv[SEQ:, SEQ:] = np.asarray(L0_xattn_Wv).T
    arrays |= {
        "wq_in": twice(L0_xattn_Wq), "wk_in": twice(L0_xattn_Wk), "wv_in": wv,
        "bq_in": column(L0_xattn_bq), "bk_in": column(L0_xattn_bk),
        "bv_in": np.tile(np.asarray(L0_xattn_bv), (P, 2)),
        "eye_in": np.ascontiguousarray(np.asarray(L0_ffn_identity).T.reshape(CH, P, D).transpose(1, 0, 2)),
    }
    nc = bacc.Bacc("TRN2", target_bir_lowering=False, num_devices=1)
    args = {n: nc.dram_tensor(n, a.shape, mybir.dt.from_np(a.dtype), kind="ExternalInput").ap()
            for n, a in arrays.items()}
    out = nc.dram_tensor("out", (B, SEQ, D), F32, kind="ExternalOutput").ap()
    decoder_layer(nc, **args, out=out)
    r = run_bass_kernel_spmd(nc, [arrays], core_ids=[0])
    return r.results[0]["out"]
```

```python
from contextlib import ExitStack

import numpy as np

import concourse.bass as bass
from concourse import mybir
from concourse.alu_op_type import AluOpType as ALU

ACT = mybir.ActivationFunctionType
AX = mybir.AxisListType
F32 = mybir.dt.float32
F32R = mybir.dt.float32r

P = 128
B, SEQ, D = 32, 64, 512
TOKENS = B * SEQ
TILES = TOKENS // P
CH = D // P
HEADS, HD = 32, 128
HG = 2
GROUPS = HEADS // HG
TB = 4
BT = TOKENS // TB
TT = BT // P
EPS = 1e-5
LAYER_IDX, N_LAYERS = 1, 32


def decay_table():
    f = np.float32
    base = f(1.0 / 2.0 ** (8.0 / HEADS))
    factor = f(1.0 - LAYER_IDX / (N_LAYERS - 1 + 1e-5) + 1e-5)
    slope = (base ** (np.arange(HEADS, dtype=f) + f(1.0)) * factor).astype(np.float64)
    m = np.arange(P)[:, None, None]
    n = np.arange(P)[None, None, :]
    seen = (n >= m) & (n // SEQ == m // SEQ)
    return np.where(seen, np.exp(-slope[None, :, None] * np.maximum(n - m, 0)), 0.0).astype(f)


class Prepared:

    def __init__(self, sb, sem, stage, ctx_in, consts):
        self.ctx_in = ctx_in
        self.consts = consts
        self.ctx = stage[:, 0:2]
        self.ctx_parts = sb("ctx_parts", [P, 2, D], F32R)
        self.mats = sb("mats", [P, 4, P])
        self.mats_hi = sb("mats_hi", [P, 4, P], F32R)
        self.mats_lo = sb("mats_lo", [P, 3, P], F32R)
        self.bqk = sb("bqk", [P, 2])
        self.wv = sb("wv", [P, P])
        self.ms = sb("ms", [P, TILES])
        self.ctx_landed = [sem(f"ctx_landed{i}") for i in range(2)]
        self.consts_landed = sem("consts_landed")
        self.mats_hi_cut = sem("mats_hi_cut")
        self.mats_cut = sem("mats_cut")
        self.ctx_hi_ready = sem("ctx_hi_ready")
        self.ctx_ready = sem("ctx_ready")
        self.summed = sem("summed")
        self.ms_ready = sem("ms_ready")


def decoder_layer(nc, x, ctx_in, w_qkv, w_gate, w_out, norm_w, decay, ident_in, wq_in, wk_in, wv_in, bq_in, bk_in,
                  bv_in, eye_in, out):
    with ExitStack() as both:
        def sb(stack, name, shape, dt=F32):
            return stack.enter_context(nc.sbuf_tensor(name, shape, dt))

        def sem(name):
            return both.enter_context(nc.semaphore(name))

        bank = both.enter_context(nc.psum_tensor("bank", [P, 8, 512], F32))
        attn_acc = sb(both, "attn_acc", [P, TILES, D])
        sq_acc = sb(both, "sq_acc", [P, TOKENS])
        ident = sb(both, "ident", [P, P])
        ones = sb(both, "ones", [P, 2])
        stage = sb(both, "stage", [P, TT, D])
        pre = Prepared(lambda name, shape, dt=F32: sb(both, name, shape, dt), sem, stage, ctx_in,
                       (wq_in, wk_in, bq_in, bk_in, wv_in, bv_in, ident_in))

        attention(nc, sb, sem, bank, attn_acc, sq_acc, ident, ones, stage, pre,
                  x, w_qkv, w_gate, w_out, norm_w, decay, ident_in)
        cross_and_ffn(nc, sb, sem, bank, attn_acc, ident, pre, x, eye_in, out)


def load_ctx(sp, pre, b, i):
    for half in range(2):
        sp.dma_start(pre.ctx[half * SEQ:(half + 1) * SEQ, i], pre.ctx_in[b]).then_inc(pre.ctx_landed[i], 16)


def cut_ctx_hi(nc, act, pre, i, nth):
    act.wait_ge(pre.ctx_landed[i], nth * 32)
    nc.scalar.activation(pre.ctx_parts[:, i], pre.ctx[:, i], ACT.Copy).then_inc(pre.ctx_hi_ready, 1)


def cut_ctx_lo(nc, pool, pre, b, i):
    pool.wait_ge(pre.ctx_hi_ready, b + 1)
    lo = slice(SEQ, P)
    nc.gpsimd.tensor_tensor(pre.ctx_parts[lo, i], pre.ctx[lo, i], pre.ctx_parts[lo, i].bitcast(F32),
                            ALU.subtract).then_inc(pre.ctx_ready, 1)
    pool.wait_ge(pre.ctx_ready, b + 1)


def wait_apart(eng, sem, value, passed):
    eng.wait_ge(sem, value)
    eng.sem_inc(passed, 1)


def attention(nc, sb, sem, bank, attn_acc, sq_acc, ident, ones, xn, pre, x, w_qkv, w_gate, w_out, norm_w, decay,
              ident_in):
    with ExitStack() as own:
        xn_hi = sb(own, "xn_hi", [P, CH, TOKENS], F32R)
        xn_lo = sb(own, "xn_lo", [P, CH, TOKENS], F32R)
        w_hi = sb(own, "w_hi", [P, 5, CH * HG * HD], F32R)
        w_lo = sb(own, "w_lo", [P, 5, CH * HG * HD], F32R)
        raw = sb(own, "raw", [P, 2, CH * HG * HD])
        decays = sb(own, "decays", [P, HG, P])
        normw = sb(own, "normw", [P, HEADS])
        qk = sb(own, "qk", [P, 2, HG, BT])
        v = sb(own, "v", [P, TT, HG * HD])
        scores = sb(own, "scores", [P, HG, BT])
        gate = sb(own, "gate", [P, HG, BT])
        attn = sb(own, "attn", [P, HG, BT])
        y_hi = sb(own, "y_hi", [P, HG, BT], F32R)
        y_lo = sb(own, "y_lo", [P, HG, BT], F32R)
        sq = sb(own, "sq", [P, BT])
        stats = sb(own, "stats", [P, 2, 6])
        mv = sb(own, "mv", [P, 2, 2])
        rstd = sb(own, "rstd", [P, 2])
        minus_half = sb(own, "minus_half", [P, 1])

        wq, wk, wv, wg, wo = range(5)

        x_tile_landed = [sem(f"x_tile_landed{i}") for i in range(TT)]
        x_landed = [sem(f"x_landed{i}") for i in range(1, TB)]
        const_landed = sem("const_landed")
        normw_landed = sem("normw_landed")
        consts_set = sem("consts_set")
        decay_landed = sem("decay_landed")
        raw_landed = [sem("raw_landed_a"), sem("raw_landed_b")]
        hi_cut = sem("hi_cut")
        w_ready = sem("w_ready")
        stats_done = sem("stats_done")
        var_ready = sem("var_ready")
        eps_added = sem("eps_added")
        rstd_ready = sem("rstd_ready")
        xn_ready = sem("xn_ready")
        xn_turned = sem("xn_turned")
        xn_hi_ready = sem("xn_hi_ready")
        xn_lo_ready = sem("xn_lo_ready")
        v_mm, s_mm, g_mm, pv_mm, qk_mm, out_mm = (sem(n) for n in ("v_mm", "s_mm", "g_mm", "pv_mm", "qk_mm", "out_mm"))
        v_sig, qk_sig, gate_ready, attn_ready = (sem(n) for n in ("v_sig", "qk_sig", "gate_ready", "attn_ready"))
        v_ready, qk_ready, scores_ready = (sem(n) for n in ("v_ready", "qk_ready", "scores_ready"))
        y_made, y_hi_ready, y_ready = (sem(n) for n in ("y_made", "y_hi_ready", "y_ready"))
        out_added = sem("out_added")
        sq_made, sq_added = sem("sq_made"), sem("sq_added")

        x_t = x.rearrange("b s d -> (b s) d").rearrange("(k t p) d -> k p t d", t=TT, p=P)

        def turn_bank(t):
            return 4 + t if t < TT else 6 + t % 2

        with nc.Block() as block:

            @block.sync
            def _(sp):
                sp.dma_start(ident[:, :], ident_in).then_inc(const_landed, 16)
                for t in range(TT):
                    sp.dma_start(attn_acc[:, t], x_t[0, :, t]).then_inc(x_tile_landed[t], 16)
                sp.dma_start(raw[:, 0], w_qkv[0, 0]).then_inc(raw_landed[0], 16)
                sp.dma_start(raw[:, 1], w_qkv[0, 1]).then_inc(raw_landed[1], 16)
                sp.dma_start(normw[:, :], norm_w).then_inc(normw_landed, 16)
                sp.dma_start(decays[:, :, :], decay[:, 0:HG, :]).then_inc(decay_landed, 16)

                def load_x(k):
                    sp.dma_start(attn_acc[:, k * TT:(k + 1) * TT], x_t[k]).then_inc(x_landed[k - 1], 16)

                def rest_of_group(g, first=False):
                    sp.wait_ge(w_ready, g * 5 + (wq + 1))
                    sp.dma_start(raw[:, 0], w_qkv[g, 2]).then_inc(raw_landed[0], 16)
                    sp.wait_ge(w_ready, g * 5 + (wk + 1))
                    sp.dma_start(raw[:, 1], w_gate[g]).then_inc(raw_landed[1], 16)
                    if first:
                        load_x(1)
                    sp.wait_ge(w_ready, g * 5 + (wv + 1))
                    sp.dma_start(raw[:, 0], w_out[g]).then_inc(raw_landed[0], 16)
                    if first:
                        load_x(2)
                        load_x(3)

                def next_group(g):
                    sp.wait_ge(w_ready, g * 5 + (wo + 1))
                    sp.dma_start(raw[:, 0], w_qkv[g + 1, 0]).then_inc(raw_landed[0], 16)
                    sp.dma_start(raw[:, 1], w_qkv[g + 1, 1]).then_inc(raw_landed[1], 16)
                    sp.wait_ge(scores_ready, (g + 1) * (TB * HG))
                    sp.dma_start(decays[:, :, :], decay[:, bass.ds((g + 1) * HG, HG), :]).then_inc(decay_landed, 16)

                rest_of_group(0, True)
                next_group(0)
                with nc.Fori(1, GROUPS - 1, engines=[sp.engine], hint_back_edge=True) as g:
                    rest_of_group(g)
                    next_group(g)
                rest_of_group(GROUPS - 1)
                for i in range(2):
                    load_ctx(sp, pre, i, i)
                for dst, src in zip((pre.mats[:, 0], pre.mats[:, 1], pre.bqk[:, 0:1], pre.bqk[:, 1:2], pre.wv[:, :],
                                     pre.mats[:, 2], pre.mats[:, 3]), pre.consts):
                    sp.dma_start(dst, src).then_inc(pre.consts_landed, 16)

            @block.gpsimd
            def _(pool):
                nc.gpsimd.memset(minus_half[:, :], -0.5).then_inc(consts_set, 1)
                nc.gpsimd.memset(ones[:, :], 1.0).then_inc(consts_set, 1)
                nc.gpsimd.memset(sq_acc[:, :], 0.0).then_inc(sq_made, HG)
                pool.wait_ge(consts_set, 2)

                def inv_roots(tb):
                    for t in range(tb * TT, (tb + 1) * TT):
                        pool.wait_ge(var_ready, t + 1)
                        nc.gpsimd.tensor_scalar(rstd[:, t % 2:t % 2 + 1], mv[:, t % 2, 1:2], EPS, None,
                                                ALU.add).then_inc(eps_added, 1)
                        pool.wait_ge(eps_added, t + 1)
                        nc.gpsimd.tensor_tensor(rstd[:, t % 2:t % 2 + 1], rstd[:, t % 2:t % 2 + 1], minus_half[:, :],
                                                ALU.pow).then_inc(rstd_ready, 1)

                def squares(g, tb, first=False):
                    for h in range(HG):
                        n = g * (TB * HG) + (tb * HG + h)
                        pool.wait_ge(attn_ready, n + 1)
                        pool.wait_ge(sq_made, n + HG)
                        if not (first and tb == 0 and h == 0):
                            pool.wait_ge(sq_added, n)
                        nc.gpsimd.tensor_tensor(sq[:, :], attn[:, h], attn[:, h], ALU.mult).then_inc(sq_made, 1)
                        pool.wait_ge(sq_made, n + HG + 1)
                        acc = sq_acc[:, tb * BT:(tb + 1) * BT]
                        nc.gpsimd.tensor_tensor(acc, acc, sq[:, :], ALU.add).then_inc(sq_added, 1)

                inv_roots(0)
                for tb in range(TB):
                    if tb + 1 < TB:
                        inv_roots(tb + 1)
                    squares(0, tb, True)
                with nc.Fori(1, GROUPS - 1, engines=[pool.engine], hint_back_edge=True) as g:
                    for tb in range(TB):
                        squares(g, tb)
                for tb in range(TB):
                    if tb == TB - 1:
                        pool.wait_ge(sq_added, TB * HG * GROUPS - HG)
                        for i in range(2):
                            cut_ctx_lo(nc, pool, pre, i, i)
                    squares(GROUPS - 1, tb)

            @block.scalar
            def _(act):
                def cut_hi(g, w):
                    ab, nth, per = ((0, (0, 0, 1, 0, 2)[w], 3) if w in (wq, wv, wo) else (1, (w - wk) // 2, 2))
                    act.wait_ge(raw_landed[ab], g * (16 * per) + 16 * (nth + 1))
                    if w == wo:
                        for h in range(HG):
                            i = nc.scalar.activation(w_hi[:, w, h * D:(h + 1) * D], raw[:, ab, h * D:(h + 1) * D],
                                                     ACT.Copy, scale=normw[:, bass.ds(g * HG + h, 1)])
                        i.then_inc(hi_cut, 1)
                    else:
                        nc.scalar.activation(w_hi[:, w], raw[:, ab], ACT.Copy).then_inc(hi_cut, 1)

                def sigmoids_qk(u):
                    for j in range(2 * HG):
                        act.wait_ge(qk_mm, u * (2 * HG) + (j + 1))
                        nc.scalar.activation(qk[:, j // HG, j % HG], bank[:, j], ACT.Sigmoid).then_inc(qk_sig, 1)

                def turned_hi(t):
                    act.wait_ge(xn_turned, t + 1)
                    nc.scalar.activation(xn_hi[:, :, t * P:(t + 1) * P],
                                         bank[:, turn_bank(t)].rearrange("p (c n) -> p c n", c=CH),
                                         ACT.Copy).then_inc(xn_hi_ready, 1)

                def step(g, tb, first=False, last=False):
                    u = g * TB + tb
                    turns = first and tb + 1 < TB
                    if tb == TB - 1 and not last:
                        act.wait_ge(v_mm, u * 2 + 1)
                        cut_hi(g + 1, wq)
                        cut_hi(g + 1, wk)
                    for j in range(2):
                        act.wait_ge(v_mm, u * 2 + (j + 1))
                        nc.scalar.activation(v[:, 2 * j:2 * j + 2], bank[:, j].rearrange("p (t n) -> p t n", t=2),
                                             ACT.Sigmoid).then_inc(v_sig, 1)
                    if turns:
                        for i in range(2):
                            turned_hi((tb + 1) * TT + i)
                    if tb == 0:
                        cut_hi(g, wo)
                    if tb == TB - 1 and not last:
                        cut_hi(g + 1, wv)
                    for h in range(HG):
                        act.wait_ge(g_mm, u * HG + (h + 1))
                        nc.scalar.activation(gate[:, h], bank[:, 4 + h], ACT.Sigmoid).then_inc(gate_ready, 1)
                        if turns and h == 0:
                            for i in range(2, TT):
                                turned_hi((tb + 1) * TT + i)
                    for h in range(HG):
                        act.wait_ge(pv_mm, u * HG + (h + 1))
                        act.wait_ge(sq_made, u * HG + (h + 1))
                        nc.scalar.activation(attn[:, h], bank[:, 6 + h], ACT.Copy).then_inc(attn_ready, 1)
                    if tb == TB - 1 and not last:
                        cut_hi(g + 1, wg)
                    for h in range(HG):
                        act.wait_ge(y_made, u * HG + (h + 1))
                        nc.scalar.activation(y_hi[:, h], gate[:, h], ACT.Copy).then_inc(y_hi_ready, 1)
                    if not (last and tb == TB - 1):
                        sigmoids_qk(u + 1)

                for t in range(TT):
                    turned_hi(t)
                    if t in (1, 2):
                        cut_hi(0, t - 1)
                cut_hi(0, wv)
                cut_hi(0, wg)
                act.wait_ge(normw_landed, 16)
                sigmoids_qk(0)
                for tb in range(TB):
                    step(0, tb, first=True)
                with nc.Fori(1, GROUPS - 1, engines=[act.engine], hint_back_edge=True) as g:
                    for tb in range(TB):
                        step(g, tb)
                for tb in range(TB):
                    if tb == TB - 1:
                        act.wait_ge(pre.consts_landed, 16 * 7)
                        nc.scalar.activation(pre.mats_hi[:, :, :], pre.mats[:, :, :], ACT.Copy)\
                            .then_inc(pre.mats_hi_cut, 1)
                        for i in range(2):
                            cut_ctx_hi(nc, act, pre, i, 1)
                    step(GROUPS - 1, tb, last=True)

            @block.vector
            def _(dve):
                def cut_lo(g, w):
                    ab = 0 if w in (wq, wv, wo) else 1
                    dve.wait_ge(hi_cut, g * 5 + (w + 1))
                    if w == wo:
                        for h in range(HG):
                            i = nc.vector.scalar_tensor_tensor(
                                out=w_lo[:, w, h * D:(h + 1) * D], in0=raw[:, ab, h * D:(h + 1) * D],
                                scalar=normw[:, bass.ds(g * HG + h, 1)],
                                in1=w_hi[:, w, h * D:(h + 1) * D].bitcast(F32), op0=ALU.mult, op1=ALU.subtract)
                    else:
                        i = nc.vector.tensor_tensor(w_lo[:, w], raw[:, ab], w_hi[:, w].bitcast(F32), ALU.subtract)
                    i.then_inc(w_ready, 1)

                def turned_lo(t):
                    dve.wait_ge(xn_hi_ready, t + 1)
                    s = slice(t * P, (t + 1) * P)
                    nc.vector.tensor_tensor(xn_lo[:, :, s], bank[:, turn_bank(t)].rearrange("p (c n) -> p c n", c=CH),
                                            xn_hi[:, :, s].bitcast(F32), ALU.subtract).then_inc(xn_lo_ready, 1)

                def statistics(t):
                    nc.vector.bn_stats(stats[:, t % 2], attn_acc[:, t]).then_inc(stats_done, 1)
                    dve.wait_ge(stats_done, t + 1)
                    nc.vector.bn_aggr(mv[:, t % 2], stats[:, t % 2]).then_inc(var_ready, 1)

                def norm_block(tb):
                    if tb:
                        dve.wait_ge(x_landed[tb - 1], 16)
                        dve.wait_ge(xn_turned, tb * TT)
                    for i in range(TT + 1):
                        if i < TT:
                            if tb == 0:
                                dve.wait_ge(x_tile_landed[i], 16)
                            statistics(tb * TT + i)
                        if i:
                            t = tb * TT + i - 1
                            dve.wait_ge(rstd_ready, t + 1)
                            nc.vector.tensor_scalar(xn[:, t % TT], attn_acc[:, t], mv[:, t % 2, 0:1],
                                                    rstd[:, t % 2:t % 2 + 1], ALU.subtract,
                                                    ALU.mult).then_inc(xn_ready, 1)

                def silus_qk(u):
                    for j in range(2 * HG):
                        dve.wait_ge(qk_sig, u * (2 * HG) + (j + 1))
                        o = qk[:, j // HG, j % HG]
                        nc.vector.tensor_tensor(o, bank[:, j], o, ALU.mult).then_inc(qk_ready, 1)

                def step(g, tb, first=False, last=False):
                    u = g * TB + tb
                    turns = first and tb + 1 < TB
                    if turns:
                        norm_block(tb + 1)
                    if tb == TB - 1 and not last:
                        cut_lo(g + 1, wq)
                        cut_lo(g + 1, wk)
                    for j in range(2):
                        dve.wait_ge(v_sig, u * 2 + (j + 1))
                        o = v[:, 2 * j:2 * j + 2]
                        nc.vector.tensor_tensor(o, bank[:, j].rearrange("p (t n) -> p t n", t=2), o,
                                                ALU.mult).then_inc(v_ready, 1)
                    if turns:
                        for i in range(2):
                            turned_lo((tb + 1) * TT + i)
                    if tb == 0:
                        cut_lo(g, wo)
                        dve.wait_ge(decay_landed, g * 16 + 16)
                    for h in range(HG):
                        dve.wait_ge(s_mm, u * HG + (h + 1))
                        nc.vector.tensor_tensor(scores[:, h].rearrange("p (t n) -> p t n", t=TT),
                                                bank[:, 2 + h].rearrange("p (t n) -> p t n", t=TT),
                                                decays[:, h:h + 1].broadcast_to([P, TT, P]),
                                                ALU.mult).then_inc(scores_ready, 1)
                    if turns:
                        for i in range(2, TT):
                            turned_lo((tb + 1) * TT + i)
                    if tb == TB - 1 and not last:
                        cut_lo(g + 1, wv)
                    for h in range(HG):
                        dve.wait_ge(attn_ready, u * HG + (h + 1))
                        nc.vector.tensor_tensor(gate[:, h], gate[:, h], attn[:, h], ALU.mult).then_inc(y_made, 1)
                    for h in range(HG):
                        dve.wait_ge(y_hi_ready, u * HG + (h + 1))
                        nc.vector.tensor_tensor(y_lo[:, h], gate[:, h], y_hi[:, h].bitcast(F32),
                                                ALU.subtract).then_inc(y_ready, 1)
                    if tb == TB - 1 and not last:
                        cut_lo(g + 1, wg)
                    if not (last and tb == TB - 1):
                        silus_qk(u + 1)
                    for i in range(TT):
                        dve.wait_ge(out_mm, u * TT + (i + 1))
                        acc = attn_acc[:, tb * TT + i]
                        if first:
                            nc.vector.tensor_copy(acc, bank[:, 4 + i]).then_inc(out_added, 1)
                        else:
                            nc.vector.tensor_tensor(acc, acc, bank[:, 4 + i], ALU.add).then_inc(out_added, 1)

                norm_block(0)
                for t in range(TT):
                    turned_lo(t)
                for w in (wq, wk, wv, wg):
                    cut_lo(0, w)
                silus_qk(0)
                for tb in range(TB):
                    step(0, tb, first=True)
                with nc.Fori(1, GROUPS - 1, engines=[dve.engine], hint_back_edge=True) as g:
                    for tb in range(TB):
                        step(g, tb)
                for tb in range(TB):
                    if tb == TB - 1:
                        dve.wait_ge(pre.mats_hi_cut, 1)
                        nc.vector.tensor_tensor(pre.mats_lo[:, :, :], pre.mats[:, 0:3],
                                                pre.mats_hi[:, 0:3].bitcast(F32), ALU.subtract)\
                            .then_inc(pre.mats_cut, 1)
                    step(GROUPS - 1, tb, last=True)
                dve.wait_ge(pre.summed, 1)
                nc.vector.tensor_scalar(pre.ms[:, :], bank[:, 0, 0:TILES], 1.0 / (HEADS * HD), EPS, ALU.mult,
                                        ALU.add).then_inc(pre.ms_ready, 1)

            @block.tensor
            def _(pe):
                def weights(half, w, c, h):
                    return half[:, w, c * HG * HD + h * HD:c * HG * HD + (h + 1) * HD]

                def project(dst, w, h, tb, done):
                    s = slice(tb * BT, (tb + 1) * BT)
                    for c in range(CH):
                        hi = weights(w_hi, w, c, h)
                        nc.tensor.matmul(dst, hi, xn_hi[:, c, s], start=(c == 0), stop=False)
                        nc.tensor.matmul(dst, hi, xn_lo[:, c, s], start=False, stop=False)
                        i = nc.tensor.matmul(dst, weights(w_lo, w, c, h), xn_hi[:, c, s],
                                             start=False, stop=(c == CH - 1))
                    i.then_inc(done, 1)

                def project_qk(g, tb):
                    for j in range(2 * HG):
                        if tb == 0 and j % HG == 0:
                            pe.wait_ge(w_ready, g * 5 + (j // HG + 1))
                        project(bank[:, j], j // HG, j % HG, tb, qk_mm)

                def turn(t):
                    pe.wait_ge(xn_ready, t + 1)
                    if t > TT and t % TT >= 2:
                        pe.wait_ge(xn_lo_ready, t - 1)
                    for c in range(CH):
                        s = slice(c * P, (c + 1) * P)
                        k = nc.tensor.transpose(bank[:, turn_bank(t), s], xn[:, t % TT, s], ident[:, :])
                    k.then_inc(xn_turned, 1)

                def sums(tiles):
                    pe.wait_ge(sq_added, TB * HG * GROUPS - (0 if tiles[-1] == TILES - 1 else HG))
                    for t in tiles:
                        k = nc.tensor.matmul(bank[:, 0, t:t + 1], sq_acc[:, t * P:(t + 1) * P], ones[:, 0:1],
                                             start=True, stop=True)
                    if tiles[-1] == TILES - 1:
                        k.then_inc(pre.summed, 1)

                def step(g, tb, first=False, last=False):
                    u = g * TB + tb
                    turns = first and tb + 1 < TB
                    pe.wait_ge(qk_ready, u * (2 * HG) + 2)
                    if tb == 0:
                        pe.wait_ge(w_ready, g * 5 + wv + 1)
                    for i in range(TT):
                        dst = bank[:, i // 2, (i % 2) * HG * HD:(i % 2 + 1) * HG * HD]
                        s = slice(tb * BT + i * P, tb * BT + (i + 1) * P)
                        for c in range(CH):
                            m = slice(c * HG * HD, (c + 1) * HG * HD)
                            nc.tensor.matmul(dst, xn_hi[:, c, s], w_hi[:, wv, m], start=(c == 0), stop=False)
                            nc.tensor.matmul(dst, xn_hi[:, c, s], w_lo[:, wv, m], start=False, stop=False)
                            k = nc.tensor.matmul(dst, xn_lo[:, c, s], w_hi[:, wv, m], start=False, stop=(c == CH - 1))
                        if i % 2:
                            k.then_inc(v_mm, 1)
                    if turns:
                        if tb:
                            pe.wait_ge(out_added, u * TT)
                        for i in range(2):
                            turn((tb + 1) * TT + i)
                    pe.wait_ge(qk_ready, u * (2 * HG) + 2 * HG)
                    for h in range(HG):
                        for i in range(TT):
                            s = slice(i * P, (i + 1) * P)
                            k = nc.tensor.matmul(bank[:, 2 + h, s], qk[:, 1, h, s], qk[:, 0, h, s],
                                                 start=True, stop=True)
                        k.then_inc(s_mm, 1)
                    if tb == 0:
                        pe.wait_ge(w_ready, g * 5 + wg + 1)
                    for h in range(HG):
                        if h == 0 and not (first and tb == 0):
                            pe.wait_ge(out_added, u * TT - 2)
                        project(bank[:, 4 + h], wg, h, tb, g_mm)
                        if turns and h == 0:
                            for i in range(2, TT):
                                turn((tb + 1) * TT + i)
                    pe.wait_ge(v_ready, u * 2 + 2)
                    if turns:
                        pe.wait_ge(xn_lo_ready, (tb + 2) * TT)
                    elif not (first and tb == 0):
                        pe.wait_ge(out_added, u * TT)
                    for h in range(HG):
                        pe.wait_ge(scores_ready, u * HG + (h + 1))
                        for i in range(TT):
                            s = slice(i * P, (i + 1) * P)
                            k = nc.tensor.matmul(bank[:, 6 + h, s], v[:, i, h * HD:(h + 1) * HD], scores[:, h, s],
                                                 start=True, stop=True)
                        k.then_inc(pv_mm, 1)
                    if not (last and tb == TB - 1):
                        project_qk(g if tb < TB - 1 else g + 1, (tb + 1) % TB)
                    else:
                        sums(range(TILES - TT))
                    if tb == 0:
                        pe.wait_ge(w_ready, g * 5 + wo + 1)
                    pe.wait_ge(y_ready, u * HG + HG)
                    for i in range(TT):
                        s = slice(i * P, (i + 1) * P)
                        for h in range(HG):
                            m = slice(h * D, (h + 1) * D)
                            nc.tensor.matmul(bank[:, 4 + i], y_hi[:, h, s], w_hi[:, wo, m], start=(h == 0), stop=False)
                            nc.tensor.matmul(bank[:, 4 + i], y_hi[:, h, s], w_lo[:, wo, m], start=False, stop=False)
                            k = nc.tensor.matmul(bank[:, 4 + i], y_lo[:, h, s], w_hi[:, wo, m],
                                                 start=False, stop=(h == HG - 1))
                        k.then_inc(out_mm, 1)

                pe.wait_ge(const_landed, 16)
                for t in range(TT):
                    turn(t)
                pe.wait_ge(xn_lo_ready, TT)
                project_qk(0, 0)
                for tb in range(TB):
                    step(0, tb, first=True)
                with nc.Fori(1, GROUPS - 1, engines=[pe.engine], hint_back_edge=True) as g:
                    for tb in range(TB):
                        step(g, tb)
                for tb in range(TB):
                    step(GROUPS - 1, tb, last=True)
                sums(range(TILES - TT, TILES))


def cross_and_ffn(nc, sb, sem, bank, x1, ident, pre, x, eye_in, out):
    with ExitStack() as own:
        xr = sb(own, "xr", [P, TILES, D])
        rrms = sb(own, "rrms", [P, TILES])
        minus_half = sb(own, "minus_half2", [P, TILES])
        q_parts = sb(own, "q_parts", [P, 2, D], F32R)
        k_hi = sb(own, "k_hi", [P, 2, D], F32R)
        k_lo = sb(own, "k_lo", [P, 2, D], F32R)
        minus_max = sb(own, "minus_max", [P, 2, CH])
        row_sum = sb(own, "row_sum", [P, 2, CH])
        row_inv = sb(own, "row_inv", [P, 2, CH])
        prob = sb(own, "prob", [P, 2, CH, D])
        probT_hi = sb(own, "probT_hi", [P, 2, D], F32R)
        probT_lo = sb(own, "probT_lo", [P, 2, D], F32R)
        xn2 = sb(own, "xn2", [P, D])
        v_hi = sb(own, "v_hi", [P, CH, 2, P], F32R)
        v_lo = sb(own, "v_lo", [P, CH, 2, P], F32R)
        xn3 = sb(own, "xn3", [P, D])
        xn3_hi = sb(own, "xn3_hi", [P, CH, P], F32R)
        xn3_lo = sb(own, "xn3_lo", [P, CH, P], F32R)
        eye = sb(own, "eye", [P, CH, D])
        eye_hi = sb(own, "eye_hi", [P, CH, D], F32R)
        eye_lo = sb(own, "eye_lo", [P, CH, D], F32R)
        stats = sb(own, "stats2", [P, 2, 6])
        mv = sb(own, "mv2", [P, 2, 2])
        rstd = sb(own, "rstd2", [P, 2])
        shift = sb(own, "shift", [P, 2])

        names = """rrms_ready x1_ready eye_landed consts_set
            eye_hi_cut eye_cut qk_mm qk_hi_ready qk_ready r_mm max_ready exp_ready inv_ready
            prob_pool prob_last turned probT_hi_ready probT_ready pv_mm x2_ready
            ln2_stats ln2_var ln2_eps ln2_root ln2_rstd xn2_ready v_mm v_hi_ready v_ready
            ln3_stats ln3_var ln3_eps ln3_root ln3_rstd xn3_ready xn3_turned xn3_hi_ready xn3T_ready
            ffn_mm out_ready stored""".split()
        S = {n: sem("cross_" + n) for n in names}
        passed = sem("passed")
        x_back = [sem(f"x_back{i}") for i in range(TB)]
        ctx_parts, mats_hi, mats_lo, bqk, wv = pre.ctx_parts, pre.mats_hi, pre.mats_lo, pre.bqk, pre.wv
        x_t = x.rearrange("b s d -> (b s) d").rearrange("(k t p) d -> k p t d", t=TT, p=P)
        out_t = out.rearrange("b s d -> (b s) d").rearrange("(t p) d -> t p d", p=P)
        PAIRS = TILES
        Q, K, OUT, MISC = 4, 5, 6, 7

        with nc.Block() as block:

            @block.sync
            def _(sp):
                def load_x(k):
                    sp.dma_start(xr[:, k * TT:(k + 1) * TT], x_t[k]).then_inc(x_back[k], 16)

                load_x(0)
                load_ctx(sp, pre, 2, 0)
                load_ctx(sp, pre, 3, 1)
                sp.dma_start(eye[:, :, :], eye_in).then_inc(S["eye_landed"], 16)
                for k in range(1, TB):
                    load_x(k)

                def store(t):
                    sp.wait_ge(S["out_ready"], t + 1)
                    sp.dma_start(out_t[t], x1[:, t]).then_inc(S["stored"], 16)

                def pair(t, first=False):
                    for i in range(2):
                        sp.wait_ge(pre.ctx_ready, t * 2 + (i + 1))
                        load_ctx(sp, pre, t * 2 + (2 + i), i)
                    if not first:
                        store(t - 2)

                pair(1, True)
                with nc.Fori(2, PAIRS - 1, engines=[sp.engine], hint_back_edge=True) as t:
                    pair(t)
                store(PAIRS - 3)
                store(PAIRS - 2)
                store(PAIRS - 1)
                sp.wait_ge(S["stored"], 16 * PAIRS)

            @block.gpsimd
            def _(pool):
                nc.gpsimd.memset(minus_half[:, :], -0.5).then_inc(S["consts_set"], 1)
                pool.wait_ge(S["consts_set"], 1)
                nc.gpsimd.tensor_tensor(rrms[:, :], pre.ms[:, :], minus_half[:, :],
                                        ALU.pow).then_inc(S["rrms_ready"], 1)
                nc.gpsimd.memset(v_hi[:, :, :, :].bitcast(F32), 0.0).then_inc(S["consts_set"], 1)
                nc.gpsimd.memset(v_lo[:, :, :, :].bitcast(F32), 0.0).then_inc(S["consts_set"], 1)
                pool.wait_ge(S["rrms_ready"], 1)
                pool.wait_ge(S["consts_set"], 3)

                def inv_root(n, k, t):
                    wait_apart(pool, S[f"ln{n}_var"], t + 1, passed)
                    nc.gpsimd.tensor_scalar(rstd[:, k:k + 1], mv[:, k, 1:2], EPS, None,
                                            ALU.add).then_inc(S[f"ln{n}_eps"], 1)
                    pool.wait_ge(S[f"ln{n}_eps"], t + 1)
                    nc.gpsimd.tensor_tensor(rstd[:, k:k + 1], rstd[:, k:k + 1], minus_half[:, 0:1],
                                            ALU.pow).then_inc(S[f"ln{n}_root"], 1)
                    wait_apart(pool, S[f"ln{n}_root"], t + 1, passed)
                    nc.gpsimd.tensor_scalar(shift[:, k:k + 1], mv[:, k, 0:1], rstd[:, k:k + 1], -1.0, ALU.mult,
                                            ALU.mult).then_inc(S[f"ln{n}_rstd"], 1)

                def normalise(b, i, tiles=range(3)):
                    for j in tiles:
                        wait_apart(pool, S["inv_ready"], b * CH + (j + 1), passed)
                        nc.gpsimd.tensor_scalar(prob[:, i, j], prob[:, i, j], row_inv[:, i, j:j + 1], None,
                                                ALU.mult).then_inc(S["prob_pool"], 1)

                def pair(t, first=False, last=False, more_pairs=True):
                    for i in range(2):
                        b = t * 2 + i
                        if not (last and i == 1):
                            normalise(b + 1, 1 - i, range(2))
                        if i == 0 and not first:
                            inv_root(3, 1, t - 1)
                        if not (last and i == 1):
                            normalise(b + 1, 1 - i, range(2, 3))
                        if i == 0 and not last or i == 1 and more_pairs:
                            pool.wait_ge(S["prob_pool"], b * 3 + 6)
                            cut_ctx_lo(nc, pool, pre, b + 3, 1 - i)
                        if i == 1 and more_pairs:
                            inv_root(2, 0, t + 2)

                cut_ctx_lo(nc, pool, pre, 2, 0)
                inv_root(2, 0, 0)
                inv_root(2, 0, 1)
                pair(0, first=True)
                with nc.Fori(1, PAIRS - 2, engines=[pool.engine], hint_back_edge=True) as t:
                    pair(t)
                pair(PAIRS - 2, more_pairs=False)
                pair(PAIRS - 1, last=True, more_pairs=False)
                inv_root(3, 1, PAIRS - 1)

            @block.scalar
            def _(act):
                def qk_hi(b, i, which=range(2), at=(Q, K)):
                    for j in which:
                        dst = (q_parts, k_hi)[j]
                        act.wait_ge(S["qk_mm"], b * 2 + (j + 1))
                        nc.scalar.activation(dst[:, i], bank[:, at[j]], ACT.Identity,
                                             bias=bqk[:, j:j + 1]).then_inc(S["qk_hi_ready"], 1)

                def normed(n, k, t, dst):
                    act.wait_ge(S[f"ln{n}_rstd"], t + 1)
                    nc.scalar.activation(dst[:, :], x1[:, t], ACT.Identity, bias=shift[:, k:k + 1],
                                         scale=rstd[:, k:k + 1]).then_inc(S[f"xn{n}_ready"], 1)

                def exps(b, i, j, at=None):
                    act.wait_ge(S["max_ready"], b * CH + (j + 1))
                    nc.scalar.activation(prob[:, i, j], bank[:, j % 2 if at is None else at], ACT.Exp,
                                         bias=minus_max[:, i, j:j + 1],
                                         accum_out=row_sum[:, i, j:j + 1]).then_inc(S["exp_ready"], 1)

                def turned_hi(b, j):
                    act.wait_ge(S["turned"], b * CH + (j + 1))
                    nc.scalar.activation(probT_hi[:, j % 2], bank[:, 2 + j % 2], ACT.Copy)\
                        .then_inc(S["probT_hi_ready"], 1)

                def v_high(t, i, first=False):
                    if i == 0:
                        act.wait_ge(S["v_mm"], t + 1)
                    else:
                        act.wait_ge(S["v_ready"], t * 2 + 1)
                        if not first:
                            act.wait_ge(S["pv_mm"], t)
                    nc.scalar.activation(v_hi[:, :, i, 0:SEQ],
                                         bank[:, MISC].rearrange("p (c b o) -> p c b o", c=CH, b=2)[:, :, i],
                                         ACT.Copy).then_inc(S["v_hi_ready"], 1)

                def xn3_high(t):
                    act.wait_ge(S["xn3_turned"], t + 1)
                    nc.scalar.activation(xn3_hi[:, :, :], bank[:, MISC].rearrange("p (c n) -> p c n", c=CH),
                                         ACT.Copy).then_inc(S["xn3_hi_ready"], 1)

                def cut_eye_hi(chunks):
                    for c in chunks:
                        act.wait_ge(S["eye_landed"], 16)
                        nc.scalar.activation(eye_hi[:, c], eye[:, c], ACT.Copy).then_inc(S["eye_hi_cut"], 1)

                def pair(t, first=False, last=False, more_pairs=True):
                    for i in range(2):
                        b = t * 2 + i
                        more = not (last and i == 1)
                        turned_hi(b, 0)
                        if i == 0:
                            v_high(t, 0)
                        if i == 1 and not first:
                            xn3_high(t - 1)
                        if more:
                            exps(b + 1, 1 - i, 1)
                        if i == 0 and not last or i == 1 and more_pairs:
                            cut_ctx_hi(nc, act, pre, 1 - i, t + (2 + i))
                        turned_hi(b, 1)
                        if not last:
                            qk_hi(b + 2, i, range(1))
                        if more:
                            exps(b + 1, 1 - i, 2)
                        if not last:
                            qk_hi(b + 2, i, range(1, 2))
                        if i == 0 and first:
                            cut_eye_hi(range(2))
                        turned_hi(b, 2)
                        if i == 0:
                            v_high(t, 1, first)
                        if more:
                            exps(b + 1, 1 - i, 3)
                        if i == 0 and not first:
                            normed(3, 1, t - 1, xn3)
                        if i == 0 and first:
                            cut_eye_hi(range(2, CH))
                        turned_hi(b, 3)
                        if i == 0 and not last:
                            normed(2, 0, t + 1, xn2)
                        if not last:
                            exps(b + 2, i, 0)

                qk_hi(0, 0)
                qk_hi(1, 1, at=(OUT, MISC))
                for j in range(CH):
                    exps(0, 0, j, at=j)
                    if j == 1:
                        cut_ctx_hi(nc, act, pre, 0, 2)
                exps(1, 1, 0)
                normed(2, 0, 0, xn2)
                act.wait_ge(S["consts_set"], 3)
                pair(0, first=True)
                with nc.Fori(1, PAIRS - 2, engines=[act.engine], hint_back_edge=True) as t:
                    pair(t)
                pair(PAIRS - 2, more_pairs=False)
                pair(PAIRS - 1, last=True, more_pairs=False)
                normed(3, 1, PAIRS - 1, xn3)
                xn3_high(PAIRS - 1)

            @block.vector
            def _(dve):
                def q_low(b, i, at=Q):
                    lo = slice(SEQ, P)
                    dve.wait_ge(S["qk_hi_ready"], b * 2 + 1)
                    nc.vector.scalar_tensor_tensor(out=q_parts[lo, i], in0=bank[lo, at], scalar=bqk[lo, 0:1],
                                                   in1=q_parts[lo, i].bitcast(F32), op0=ALU.add,
                                                   op1=ALU.subtract).then_inc(S["qk_ready"], 1)

                def k_low(b, i, at=K):
                    dve.wait_ge(S["qk_hi_ready"], b * 2 + 2)
                    nc.vector.scalar_tensor_tensor(out=k_lo[:, i], in0=bank[:, at], scalar=bqk[:, 1:2],
                                                   in1=k_hi[:, i].bitcast(F32), op0=ALU.add,
                                                   op1=ALU.subtract).then_inc(S["qk_ready"], 1)

                def row_max(b, i, j, at=None):
                    dve.wait_ge(S["r_mm"], b * CH + (j + 1))
                    nc.vector.tensor_reduce(minus_max[:, i, j:j + 1], bank[:, j % 2 if at is None else at], AX.X,
                                            ALU.max, negate=True).then_inc(S["max_ready"], 1)

                def inverse(b, i, j):
                    dve.wait_ge(S["exp_ready"], b * CH + (j + 1))
                    nc.vector.reciprocal(row_inv[:, i, j:j + 1], row_sum[:, i, j:j + 1]).then_inc(S["inv_ready"], 1)

                def normalise(b, i):
                    dve.wait_ge(S["inv_ready"], b * CH + CH)
                    nc.vector.tensor_scalar(prob[:, i, 3], prob[:, i, 3], row_inv[:, i, 3:4], None,
                                            ALU.mult).then_inc(S["prob_last"], 1)

                def turned_lo(b, j):
                    dve.wait_ge(S["probT_hi_ready"], b * CH + (j + 1))
                    nc.vector.tensor_tensor(probT_lo[:, j % 2], bank[:, 2 + j % 2], probT_hi[:, j % 2].bitcast(F32),
                                            ALU.subtract).then_inc(S["probT_ready"], 1)

                def make_x1(t):
                    nc.vector.scalar_tensor_tensor(out=x1[:, t], in0=x1[:, t], scalar=rrms[:, bass.ds(t, 1)],
                                                   in1=xr[:, t], op0=ALU.mult, op1=ALU.add)\
                        .then_inc(S["x1_ready"], 1)
                    wait_apart(dve, S["x1_ready"], t + 1, passed)

                def layernorm(n, k, t):
                    nc.vector.bn_stats(stats[:, k], x1[:, t]).then_inc(S[f"ln{n}_stats"], 1)
                    wait_apart(dve, S[f"ln{n}_stats"], t + 1, passed)
                    nc.vector.bn_aggr(mv[:, k], stats[:, k]).then_inc(S[f"ln{n}_var"], 1)

                def xn3_low(t):
                    dve.wait_ge(S["xn3_hi_ready"], t + 1)
                    nc.vector.tensor_tensor(xn3_lo[:, :, :], bank[:, MISC].rearrange("p (c n) -> p c n", c=CH),
                                            xn3_hi[:, :, :].bitcast(F32), ALU.subtract).then_inc(S["xn3T_ready"], 1)

                def add_cross(t):
                    dve.wait_ge(S["pv_mm"], t + 1)
                    nc.vector.tensor_tensor(x1[:, t], x1[:, t], bank[:, OUT], ALU.add).then_inc(S["x2_ready"], 1)
                    wait_apart(dve, S["x2_ready"], t + 1, passed)

                def cut_eye_lo(chunks):
                    for c in chunks:
                        dve.wait_ge(S["eye_hi_cut"], c + 1)
                        nc.vector.tensor_tensor(eye_lo[:, c], eye[:, c], eye_hi[:, c].bitcast(F32),
                                                ALU.subtract).then_inc(S["eye_cut"], 1)

                def add_ffn(t):
                    dve.wait_ge(S["ffn_mm"], t + 1)
                    nc.vector.tensor_tensor(x1[:, t], x1[:, t], bank[:, MISC], ALU.add).then_inc(S["out_ready"], 1)

                def v_low(t, i):
                    dve.wait_ge(S["v_hi_ready"], t * 2 + (i + 1))
                    nc.vector.tensor_tensor(v_lo[:, :, i, 0:SEQ],
                                            bank[:, MISC].rearrange("p (c b o) -> p c b o", c=CH, b=2)[:, :, i],
                                            v_hi[:, :, i, 0:SEQ].bitcast(F32), ALU.subtract).then_inc(S["v_ready"], 1)

                def pair(t, first=False, last=False, more_pairs=True):
                    for i in range(2):
                        b = t * 2 + i
                        more = not (last and i == 1)
                        if more:
                            inverse(b + 1, 1 - i, 0)
                            row_max(b + 1, 1 - i, 1)
                        turned_lo(b, 0)
                        if i == 0:
                            v_low(t, 0)
                        if i == 0 and not first:
                            add_cross(t - 1)
                        if i == 1 and not first:
                            xn3_low(t - 1)
                        if i == 1 and more_pairs:
                            wait_apart(dve, S["xn2_ready"], t + 2, passed)
                            layernorm(2, 0, t + 2)
                        if more:
                            inverse(b + 1, 1 - i, 1)
                            row_max(b + 1, 1 - i, 2)
                        turned_lo(b, 1)
                        if not last:
                            q_low(b + 2, i)
                        if i == 0 and not first:
                            layernorm(3, 1, t - 1)
                        if not last:
                            k_low(b + 2, i)
                        if more:
                            inverse(b + 1, 1 - i, 2)
                            row_max(b + 1, 1 - i, 3)
                        turned_lo(b, 2)
                        if i == 0:
                            v_low(t, 1)
                        if i == 1 and not first:
                            add_ffn(t - 1)
                        if i == 1 and first:
                            cut_eye_lo(range(2))
                        if more:
                            inverse(b + 1, 1 - i, 3)
                            normalise(b + 1, 1 - i)
                        if not last:
                            row_max(b + 2, i, 0)
                        turned_lo(b, 3)
                        if i == 0 and more_pairs:
                            make_x1(t + 2)
                        if i == 1 and first:
                            cut_eye_lo(range(2, CH))

                q_low(0, 0)
                k_low(0, 0)
                for j in range(CH):
                    row_max(0, 0, j, at=j)
                q_low(1, 1, at=OUT)
                k_low(1, 1, at=MISC)
                dve.wait_ge(S["rrms_ready"], 1)
                dve.wait_ge(x_back[0], 16)
                make_x1(0)
                layernorm(2, 0, 0)
                for j in range(CH):
                    inverse(0, 0, j)
                    dve.wait_ge(S["inv_ready"], j + 1)
                    nc.vector.tensor_scalar(prob[:, 0, j], prob[:, 0, j], row_inv[:, 0, j:j + 1], None, ALU.mult)\
                        .then_inc(S["prob_last"] if j == CH - 1 else S["prob_pool"], 1)
                row_max(1, 1, 0)
                make_x1(1)
                dve.wait_ge(S["xn2_ready"], 1)
                layernorm(2, 0, 1)
                pair(0, first=True)
                for k in range(1, TB):
                    dve.wait_ge(x_back[k], 16)
                with nc.Fori(1, PAIRS - 2, engines=[dve.engine], hint_back_edge=True) as t:
                    pair(t)
                pair(PAIRS - 2, more_pairs=False)
                pair(PAIRS - 1, last=True, more_pairs=False)
                add_cross(PAIRS - 1)
                layernorm(3, 1, PAIRS - 1)
                xn3_low(PAIRS - 1)
                add_ffn(PAIRS - 1)

            @block.tensor
            def _(pe):
                def project(b, i, at=(Q, K)):
                    pe.wait_ge(pre.ctx_ready, b + 1)
                    for j in range(2):
                        nc.tensor.matmul(bank[:, at[j]], mats_hi[:, j], ctx_parts[:, i], start=True, stop=False)
                        nc.tensor.matmul(bank[:, at[j]], mats_lo[:, j], ctx_parts[:, i], start=False,
                                         stop=True).then_inc(S["qk_mm"], 1)

                def cross_scores(b, i, j, at=None):
                    if at is None:
                        at = j % 2
                        pe.wait_ge(S["exp_ready"], b * CH + (j - 1))
                    if j == 0:
                        pe.wait_ge(S["qk_ready"], b * 2 + 2)
                    q = q_parts[:, i, j * P:(j + 1) * P]
                    nc.tensor.matmul(bank[:, at], q, k_hi[:, i], start=True, stop=False)
                    nc.tensor.matmul(bank[:, at], q, k_lo[:, i], start=False, stop=True).then_inc(S["r_mm"], 1)

                def turn(b, i, j):
                    if j == 0:
                        pe.wait_ge(S["prob_pool"], b * 3 + 3)
                        pe.wait_ge(S["prob_last"], b + 1)
                    for k in range(CH):
                        m = nc.tensor.transpose(bank[:, 2 + j % 2, k * P:(k + 1) * P],
                                                prob[:, i, k, j * P:(j + 1) * P], ident[:, :])
                    m.then_inc(S["turned"], 1)

                def weigh(b, i, j):
                    pe.wait_ge(S["probT_ready"], b * CH + (j + 1))
                    cols = slice(i * SEQ, i * SEQ + P)
                    vh = v_hi[:, j].rearrange("p b o -> p (b o)")[:, cols]
                    vl = v_lo[:, j].rearrange("p b o -> p (b o)")[:, cols]
                    nc.tensor.matmul(bank[:, OUT], vh, probT_hi[:, j % 2], start=(i == 0 and j == 0), stop=False)
                    nc.tensor.matmul(bank[:, OUT], vh, probT_lo[:, j % 2], start=False, stop=False)
                    m = nc.tensor.matmul(bank[:, OUT], vl, probT_hi[:, j % 2], start=False,
                                         stop=(i == 1 and j == CH - 1))
                    if i == 1 and j == CH - 1:
                        m.then_inc(S["pv_mm"], 1)

                def values(t, first=False):
                    pe.wait_ge(S["xn2_ready"], t + 1)
                    if not first:
                        pe.wait_ge(S["out_ready"], t - 1)
                    for part in (mats_hi, mats_lo):
                        nc.tensor.matmul(bank[:, MISC].rearrange("p (c n) -> p c n", c=CH), mats_hi[:, 3],
                                         part[:, 2:3].broadcast_to([P, CH, P]), start=part is mats_hi, stop=False)
                    for c in range(CH):
                        m = nc.tensor.matmul(bank[:, MISC, c * P:(c + 1) * P], xn2[:, c * P:(c + 1) * P], wv[:, :],
                                             start=False, stop=(c == CH - 1))
                    m.then_inc(S["v_mm"], 1)

                def turn_xn3(t):
                    pe.wait_ge(S["xn3_ready"], t + 1)
                    for c in range(CH):
                        s = slice(c * P, (c + 1) * P)
                        m = nc.tensor.transpose(bank[:, MISC, s], xn3[:, s], ident[:, :])
                    m.then_inc(S["xn3_turned"], 1)

                def ffn(t, chunks=range(CH)):
                    if 0 in chunks:
                        pe.wait_ge(S["eye_cut"], CH)
                        pe.wait_ge(S["xn3T_ready"], t + 1)
                    for c in chunks:
                        nc.tensor.matmul(bank[:, MISC], xn3_hi[:, c], eye_hi[:, c], start=(c == 0), stop=False)
                        nc.tensor.matmul(bank[:, MISC], xn3_hi[:, c], eye_lo[:, c], start=False, stop=False)
                        m = nc.tensor.matmul(bank[:, MISC], xn3_lo[:, c], eye_hi[:, c], start=False,
                                             stop=(c == CH - 1))
                    if CH - 1 in chunks:
                        m.then_inc(S["ffn_mm"], 1)

                def pair(t, first=False, last=False):
                    for i in range(2):
                        b = t * 2 + i
                        more = not (last and i == 1)
                        for j in range(CH):
                            if j < CH - 1 and more:
                                cross_scores(b + 1, 1 - i, j + 1)
                            turn(b, i, j)
                            if j == CH - 1 and not last:
                                cross_scores(b + 2, i, 0)
                            if j == 0 and not (first and i == 0):
                                weigh(b - 1, 1 - i, CH - 1)
                            if j == 0 and not last:
                                project(b + 2, i)
                            if (i, j) == (0, 0) and first:
                                values(0, True)
                            if j == 1:
                                pe.wait_ge(S["v_ready"], t * 2 + (i + 1))
                                if i == 0 and not first:
                                    pe.wait_ge(S["x2_ready"], t)
                            if j:
                                weigh(b, i, j - 1)
                            if (i, j) == (0, 3) and not first:
                                pe.wait_ge(S["v_ready"], t * 2 + 2)
                                turn_xn3(t - 1)
                            if i == 1 and j in (1, 2) and not first:
                                ffn(t - 1, range(CH // 2 * (j - 1), CH // 2 * j))
                            if (i, j) == (1, 3) and not last:
                                values(t + 1, first)

                project(0, 0)
                project(1, 1, at=(OUT, MISC))
                for j in range(CH):
                    cross_scores(0, 0, j, at=j)
                cross_scores(1, 1, 0)
                pair(0, first=True)
                with nc.Fori(1, PAIRS - 1, engines=[pe.engine], hint_back_edge=True) as t:
                    pair(t)
                pair(PAIRS - 1, last=True)
                weigh(2 * PAIRS - 1, 1, CH - 1)
                turn_xn3(PAIRS - 1)
                ffn(PAIRS - 1)


def kernel(x, ctx_4096, L0_attn_qkv_w, L0_attn_out_w, L0_attn_gate_w, L0_attn_norm_w, L0_xattn_Wq, L0_xattn_bq,
           L0_xattn_Wk, L0_xattn_bk, L0_xattn_Wv, L0_xattn_bv, L0_ffn_identity):
    import concourse.bacc as bacc
    from concourse.bass_utils import run_bass_kernel_spmd

    def rows(w):
        w = w.reshape(GROUPS, HG, HD, CH, P).transpose(0, 4, 3, 1, 2)
        return np.ascontiguousarray(w.reshape(GROUPS, P, CH * HG * HD))

    qkv = np.asarray(L0_attn_qkv_w).reshape(HEADS, 3, HD, D)
    arrays = {
        "x": np.asarray(x),
        "ctx_in": np.asarray(ctx_4096),
        "w_qkv": np.ascontiguousarray(np.stack([rows(qkv[:, i]) for i in range(3)], axis=1)),
        "w_gate": rows(np.asarray(L0_attn_gate_w)),
        "w_out": np.ascontiguousarray(np.asarray(L0_attn_out_w).reshape(D, GROUPS, HG, HD).transpose(1, 3, 2, 0)
                                      .reshape(GROUPS, HD, HG * D)),
        "norm_w": np.ascontiguousarray(np.asarray(L0_attn_norm_w).reshape(HEADS, HD).T),
        "decay": decay_table(),
        "ident_in": np.eye(P, dtype=np.float32),
    }
    twice = lambda w: np.tile(np.asarray(w).T, (2, 2))
    column = lambda v: np.ascontiguousarray(np.tile(np.asarray(v), 2)[:, None])
    wv = np.zeros((P, P), np.float32)
    wv[:SEQ, :SEQ] = wv[SEQ:, SEQ:] = np.asarray(L0_xattn_Wv).T
    arrays |= {
        "wq_in": twice(L0_xattn_Wq), "wk_in": twice(L0_xattn_Wk), "wv_in": wv,
        "bq_in": column(L0_xattn_bq), "bk_in": column(L0_xattn_bk),
        "bv_in": np.tile(np.asarray(L0_xattn_bv), (P, 2)),
        "eye_in": np.ascontiguousarray(np.asarray(L0_ffn_identity).T.reshape(CH, P, D).transpose(1, 0, 2)),
    }
    nc = bacc.Bacc("TRN2", target_bir_lowering=False, num_devices=1)
    args = {n: nc.dram_tensor(n, a.shape, mybir.dt.from_np(a.dtype), kind="ExternalInput").ap()
            for n, a in arrays.items()}
    out = nc.dram_tensor("out", (B, SEQ, D), F32, kind="ExternalOutput").ap()
    decoder_layer(nc, **args, out=out)
    r = run_bass_kernel_spmd(nc, [arrays], core_ids=[0])
    return r.results[0]["out"]
```
